# Optimizing a Trainium2 kernel written in Bass

```python
import numpy as np
import jax
import jax.numpy as jnp

def _softmax(x, axis=-1):
    return jax.nn.softmax(x, axis=axis)

def _gelu(x):
    return jax.nn.gelu(x, approximate=True)

def _silu(x):
    return jax.nn.silu(x)

def _sigmoid(x):
    return jax.nn.sigmoid(x)

def _layernorm(x, axis=-1, eps=1e-05):
    m = jnp.mean(x, axis=axis, keepdims=True)
    v = jnp.var(x, axis=axis, keepdims=True)
    return (x - m) / jnp.sqrt(v + eps)

def _scatter_add(tgt, idx, src, axis=0):
    return tgt.at[idx].add(src)

def _segment_sum(src, seg, n):
    return jax.ops.segment_sum(src, seg, n)
kernel_name = 'mk_conv_preact_d2_conv_nchw128_r2_6216d5'

def setup_inputs(seed: int=0):
    np.random.seed(seed)
    _w = jnp.asarray

    def _rec_inputs():
        import jax
        import jax.numpy as jnp
        _gk = jax.random.key(seed)
        x = -0.0003929 + 0.9999 * jax.random.normal(jax.random.fold_in(_gk, 1), (2, 64, 128, 128), jnp.float32)
        return x
    x = _rec_inputs()

    def _L0_conv_setup():
        import jax, jax.numpy as jnp
        import numpy as np
        from jax import lax
        BN_EPS = 0.001
        BN_S = float(1.0 / np.sqrt(1.0 + BN_EPS))
        DN = ('NCHW', 'OIHW', 'NCHW')

        def conv3(x, w, stride):
            return lax.conv_general_dilated(x, w, (stride, stride), [(1, 1), (1, 1)], dimension_numbers=DN)

        def conv1x1(x, w, stride):
            return lax.conv_general_dilated(x, w, (stride, stride), [(0, 0), (0, 0)], dimension_numbers=DN)

        def deconv2(x, w):
            n, c, h, wd = x.shape
            y = jnp.einsum('nchw,cokl->nohkwl', x, w)
            return y.reshape(n, w.shape[1], 2 * h, 2 * wd)

        def basic_block(x, w1, w2, stride=1, ds=None):
            out = jax.nn.relu(conv3(x, w1, stride) * BN_S)
            out = conv3(out, w2, 1) * BN_S
            identity = conv1x1(x, ds, stride) * BN_S if ds is not None else x
            return jax.nn.relu(out + identity)
        key = jax.random.key(seed)
        ks = jax.random.split(key, 18)
        D = 64
        w33 = lambda k: jax.random.normal(k, (D, D, 3, 3), jnp.float32) * 0.04
        w11 = lambda k: jax.random.normal(k, (D, D, 1, 1), jnp.float32) * 0.12
        wT = lambda k: jax.random.normal(k, (D, D, 2, 2), jnp.float32) * 0.06
        return {'x': jax.random.normal(ks[0], (2, D, 128, 128), jnp.float32), 'e0b0c1': w33(ks[1]), 'e0b0c2': w33(ks[2]), 'e0b1c1': w33(ks[3]), 'e0b1c2': w33(ks[4]), 'e1b0c1': w33(ks[5]), 'e1b0c2': w33(ks[6]), 'e1b0ds': w11(ks[7]), 'e1b1c1': w33(ks[8]), 'e1b1c2': w33(ks[9]), 'e2b0c1': w33(ks[10]), 'e2b0c2': w33(ks[11]), 'e2b0ds': w11(ks[12]), 'e2b1c1': w33(ks[13]), 'e2b1c2': w33(ks[14]), 'dec0w': wT(ks[15]), 'dec1w': wT(ks[16])}
    _L0_conv_all = _L0_conv_setup()
    _L0_conv_in = {k: v for k, v in _L0_conv_all.items() if k in ('e0b0c1', 'e0b0c2', 'e0b1c1', 'e0b1c2', 'e1b0c1', 'e1b0c2', 'e1b0ds', 'e1b1c1', 'e1b1c2', 'e2b0c1', 'e2b0c2', 'e2b0ds', 'e2b1c1', 'e2b1c2', 'dec0w', 'dec1w')}
    del _L0_conv_all

    def _L1_conv_setup():
        import jax, jax.numpy as jnp
        import numpy as np
        K = 3
        PAD = 1
        STRIDE = 1

        def _conv2d(x, w, b, stride, pad):
            y = jax.lax.conv_general_dilated(x, w, window_strides=(stride, stride), padding=[(pad, pad), (pad, pad)], dimension_numbers=('NCHW', 'OIHW', 'NCHW'))
            return y + b[None, :, None, None]

        def _deform_conv(x, offsets, w_def, stride, pad):
            B, C, H, W = x.shape
            Cout = w_def.shape[0]
            Ho, Wo = (offsets.shape[2], offsets.shape[3])
            K2 = K * K
            off = offsets.reshape(B, K2, 2, Ho, Wo)
            dy, dx = (off[:, :, 0], off[:, :, 1])
            k = jnp.arange(K2)
            iy = (k // K).astype(x.dtype)
            ix = (k % K).astype(x.dtype)
            hs = (jnp.arange(Ho) * stride - pad).astype(x.dtype)
            ws = (jnp.arange(Wo) * stride - pad).astype(x.dtype)
            py = hs[None, None, :, None] + iy[None, :, None, None] + dy
            px = ws[None, None, None, :] + ix[None, :, None, None] + dx
            y0 = jnp.floor(py)
            x0 = jnp.floor(px)
            wy = py - y0
            wx = px - x0
            x_flat = x.reshape(B, C, H * W)

            def gather(yi, xi, wgt):
                valid = (yi >= 0) & (yi < H) & (xi >= 0) & (xi < W)
                yic = jnp.clip(yi, 0, H - 1).astype(jnp.int32)
                xic = jnp.clip(xi, 0, W - 1).astype(jnp.int32)
                idx = (yic * W + xic).reshape(B, -1)
                g = jax.vmap(lambda xf, i: xf[:, i])(x_flat, idx)
                return g * (wgt * valid).reshape(B, 1, -1)
            val = gather(y0, x0, (1 - wy) * (1 - wx))
            val = val + gather(y0, x0 + 1, (1 - wy) * wx)
            val = val + gather(y0 + 1, x0, wy * (1 - wx))
            val = val + gather(y0 + 1, x0 + 1, wy * wx)
            val = val.reshape(B, C, K2, Ho, Wo)
            return jnp.einsum('bckhw,ock->bohw', val, w_def.reshape(Cout, C, K2))
        key = jax.random.key(seed)
        k1, k2, k3, k4 = jax.random.split(key, 4)
        B, C, H, W, Cout = (8, 64, 32, 32, 64)
        x = jax.random.normal(k1, (B, C, H, W), dtype=jnp.float32)
        w_off = jax.random.normal(k2, (2 * K * K, C, K, K), dtype=jnp.float32) * 0.01
        b_off = jax.random.normal(k3, (2 * K * K,), dtype=jnp.float32) * 0.01
        w_def = jax.random.normal(k4, (Cout, C, K, K), dtype=jnp.float32) * (1.0 / np.sqrt(C * K * K))
        return {'x': x, 'w_off': w_off, 'b_off': b_off, 'w_def': w_def}
    _L1_conv_all = _L1_conv_setup()
    _L1_conv_in = {k: v for k, v in _L1_conv_all.items() if k in ('w_off', 'b_off', 'w_def')}
    del _L1_conv_all
    return {'x': x, 'L0_conv_e0b0c1': _L0_conv_in['e0b0c1'], 'L0_conv_e0b0c2': _L0_conv_in['e0b0c2'], 'L0_conv_e0b1c1': _L0_conv_in['e0b1c1'], 'L0_conv_e0b1c2': _L0_conv_in['e0b1c2'], 'L0_conv_e1b0c1': _L0_conv_in['e1b0c1'], 'L0_conv_e1b0c2': _L0_conv_in['e1b0c2'], 'L0_conv_e1b0ds': _L0_conv_in['e1b0ds'], 'L0_conv_e1b1c1': _L0_conv_in['e1b1c1'], 'L0_conv_e1b1c2': _L0_conv_in['e1b1c2'], 'L0_conv_e2b0c1': _L0_conv_in['e2b0c1'], 'L0_conv_e2b0c2': _L0_conv_in['e2b0c2'], 'L0_conv_e2b0ds': _L0_conv_in['e2b0ds'], 'L0_conv_e2b1c1': _L0_conv_in['e2b1c1'], 'L0_conv_e2b1c2': _L0_conv_in['e2b1c2'], 'L0_conv_dec0w': _L0_conv_in['dec0w'], 'L0_conv_dec1w': _L0_conv_in['dec1w'], 'L1_conv_w_off': _L1_conv_in['w_off'], 'L1_conv_b_off': _L1_conv_in['b_off'], 'L1_conv_w_def': _L1_conv_in['w_def']}

def reference(x, L0_conv_e0b0c1, L0_conv_e0b0c2, L0_conv_e0b1c1, L0_conv_e0b1c2, L0_conv_e1b0c1, L0_conv_e1b0c2, L0_conv_e1b0ds, L0_conv_e1b1c1, L0_conv_e1b1c2, L0_conv_e2b0c1, L0_conv_e2b0c2, L0_conv_e2b0ds, L0_conv_e2b1c1, L0_conv_e2b1c2, L0_conv_dec0w, L0_conv_dec1w, L1_conv_w_off, L1_conv_b_off, L1_conv_w_def):
    import jax
    import jax.numpy as jnp

    def _L0_conv_ref(x, e0b0c1, e0b0c2, e0b1c1, e0b1c2, e1b0c1, e1b0c2, e1b0ds, e1b1c1, e1b1c2, e2b0c1, e2b0c2, e2b0ds, e2b1c1, e2b1c2, dec0w, dec1w):
        import jax, jax.numpy as jnp
        import numpy as np
        from jax import lax
        BN_EPS = 0.001
        BN_S = float(1.0 / np.sqrt(1.0 + BN_EPS))
        DN = ('NCHW', 'OIHW', 'NCHW')

        def conv3(x, w, stride):
            return lax.conv_general_dilated(x, w, (stride, stride), [(1, 1), (1, 1)], dimension_numbers=DN)

        def conv1x1(x, w, stride):
            return lax.conv_general_dilated(x, w, (stride, stride), [(0, 0), (0, 0)], dimension_numbers=DN)

        def deconv2(x, w):
            n, c, h, wd = x.shape
            y = jnp.einsum('nchw,cokl->nohkwl', x, w)
            return y.reshape(n, w.shape[1], 2 * h, 2 * wd)

        def basic_block(x, w1, w2, stride=1, ds=None):
            out = jax.nn.relu(conv3(x, w1, stride) * BN_S)
            out = conv3(out, w2, 1) * BN_S
            identity = conv1x1(x, ds, stride) * BN_S if ds is not None else x
            return jax.nn.relu(out + identity)
        x = basic_block(x, e0b0c1, e0b0c2)
        x = basic_block(x, e0b1c1, e0b1c2)
        f0 = x
        x = basic_block(x, e1b0c1, e1b0c2, stride=2, ds=e1b0ds)
        x = basic_block(x, e1b1c1, e1b1c2)
        f1 = x
        x = basic_block(x, e2b0c1, e2b0c2, stride=2, ds=e2b0ds)
        x = basic_block(x, e2b1c1, e2b1c2)
        x = (jax.nn.relu(deconv2(x, dec0w) * BN_S) + f1) * BN_S
        x = (jax.nn.relu(deconv2(x, dec1w) * BN_S) + f0) * BN_S
        return x

    def _L1_conv_ref(x, w_off, b_off, w_def):
        import jax, jax.numpy as jnp
        import numpy as np
        K = 3
        PAD = 1
        STRIDE = 1

        def _conv2d(x, w, b, stride, pad):
            y = jax.lax.conv_general_dilated(x, w, window_strides=(stride, stride), padding=[(pad, pad), (pad, pad)], dimension_numbers=('NCHW', 'OIHW', 'NCHW'))
            return y + b[None, :, None, None]

        def _deform_conv(x, offsets, w_def, stride, pad):
            B, C, H, W = x.shape
            Cout = w_def.shape[0]
            Ho, Wo = (offsets.shape[2], offsets.shape[3])
            K2 = K * K
            off = offsets.reshape(B, K2, 2, Ho, Wo)
            dy, dx = (off[:, :, 0], off[:, :, 1])
            k = jnp.arange(K2)
            iy = (k // K).astype(x.dtype)
            ix = (k % K).astype(x.dtype)
            hs = (jnp.arange(Ho) * stride - pad).astype(x.dtype)
            ws = (jnp.arange(Wo) * stride - pad).astype(x.dtype)
            py = hs[None, None, :, None] + iy[None, :, None, None] + dy
            px = ws[None, None, None, :] + ix[None, :, None, None] + dx
            y0 = jnp.floor(py)
            x0 = jnp.floor(px)
            wy = py - y0
            wx = px - x0
            x_flat = x.reshape(B, C, H * W)

            def gather(yi, xi, wgt):
                valid = (yi >= 0) & (yi < H) & (xi >= 0) & (xi < W)
                yic = jnp.clip(yi, 0, H - 1).astype(jnp.int32)
                xic = jnp.clip(xi, 0, W - 1).astype(jnp.int32)
                idx = (yic * W + xic).reshape(B, -1)
                g = jax.vmap(lambda xf, i: xf[:, i])(x_flat, idx)
                return g * (wgt * valid).reshape(B, 1, -1)
            val = gather(y0, x0, (1 - wy) * (1 - wx))
            val = val + gather(y0, x0 + 1, (1 - wy) * wx)
            val = val + gather(y0 + 1, x0, wy * (1 - wx))
            val = val + gather(y0 + 1, x0 + 1, wy * wx)
            val = val.reshape(B, C, K2, Ho, Wo)
            return jnp.einsum('bckhw,ock->bohw', val, w_def.reshape(Cout, C, K2))
        offsets = _conv2d(x, w_off, b_off, STRIDE, PAD)
        return _deform_conv(x, offsets, w_def, STRIDE, PAD)

    def _gn(v, G=32, eps=1e-05):
        B_, C_, H_, W_ = v.shape
        g = v.reshape(B_, G, C_ // G, H_, W_)
        m = jnp.mean(g, axis=(2, 3, 4), keepdims=True)
        s = jnp.var(g, axis=(2, 3, 4), keepdims=True)
        return ((g - m) / jnp.sqrt(s + eps)).reshape(v.shape)

    def _ln_c(v, eps=1e-06):
        m = jnp.mean(v, axis=1, keepdims=True)
        s = jnp.var(v, axis=1, keepdims=True)
        return (v - m) / jnp.sqrt(s + eps)

    def _ln_t(v, eps=1e-05):
        m = jnp.mean(v, axis=-1, keepdims=True)
        s = jnp.var(v, axis=-1, keepdims=True)
        return (v - m) / jnp.sqrt(s + eps)

    def _to_tokens(v):
        B_, C_, H_, W_ = v.shape
        return v.reshape(B_, C_, H_ * W_).transpose(0, 2, 1)

    def _from_tokens(t, like):
        B_, C_, H_, W_ = like.shape
        return t.transpose(0, 2, 1).reshape(B_, C_, H_, W_)
    x = x + _L0_conv_ref(_gn(x), L0_conv_e0b0c1, L0_conv_e0b0c2, L0_conv_e0b1c1, L0_conv_e0b1c2, L0_conv_e1b0c1, L0_conv_e1b0c2, L0_conv_e1b0ds, L0_conv_e1b1c1, L0_conv_e1b1c2, L0_conv_e2b0c1, L0_conv_e2b0c2, L0_conv_e2b0ds, L0_conv_e2b1c1, L0_conv_e2b1c2, L0_conv_dec0w, L0_conv_dec1w)
    x = x + _L1_conv_ref(_gn(x), L1_conv_w_off, L1_conv_b_off, L1_conv_w_def)
    return x

_drawn_inputs = setup_inputs


def setup_inputs(seed=0):
    import zlib

    import numpy as np

    out = dict(_drawn_inputs(seed))
    spreads = {}
    factors = {'L0_conv_e2b0c1': 2.736,
     'L0_conv_e2b0c2': 2.732,
     'L0_conv_e2b1c1': 3.601,
     'L0_conv_e2b1c2': 3.054,
     'L1_conv_b_off': 7.295}
    for name, (base, spread) in spreads.items():
        noise = np.random.default_rng([zlib.crc32(name.encode()), seed]).standard_normal(out[name].shape)
        drawn = base * np.exp(spread * noise) if base else spread * noise
        out[name] = jnp.asarray(drawn.astype(out[name].dtype))
    for name, factor in factors.items():
        out[name] = (out[name] * factor).astype(out[name].dtype)
    return out
```

```python
from contextlib import ExitStack

import numpy as np
import concourse.bass as bass
from concourse import mybir

F32 = mybir.dt.float32
BF16 = mybir.dt.bfloat16
I32 = mybir.dt.int32
ACT = mybir.ActivationFunctionType
ALU = mybir.AluOpType
AX = mybir.AxisListType

P = 128
BN_S = float(1.0 / np.sqrt(1.0 + 0.001))
IMAGES, CH, H0, W0 = 2, 64, 128, 128
BANK = 512
RING = 4
GN_EPS = 1e-5
CROSS = 3

K = 3
TAPS = K * K
PS = 4
REACH = 2
HALO = REACH + 1
WIN = PS + 2 * HALO
WPX = WIN * WIN
PADW = W0 + 2 * HALO
PADH = H0 + 2 * HALO
STRIPS = H0 // PS
PATCHES = W0 // PS
OFFC = 2 * TAPS
PARTS = 3
BC_K = PARTS * OFFC + 3
ODD_AT = 32

CONV1 = ["e0b0c1", "e0b0c2", "e0b1c1", "e0b1c2", "e1b0c2", "e1b1c1", "e1b1c2", "e2b0c2", "e2b1c1", "e2b1c2"]
CONV2 = ["e1b0c1", "e2b0c1"]


UNITS = IMAGES * TAPS
DIST_RING = 6
POOL_UNITS = [n for n in range(UNITS) if n % 3 != 2]
DVE_UNITS = [n for n in range(UNITS) if n % 3 == 2]
GROUP = 3
GROUPS = -(-PATCHES // GROUP)
SUM_BANK = 6
VAL_BANKS = (4, 5, 7)


YSTEP = 8
CHUNKS = H0 // YSTEP
TILES8 = H0 // 8


class Level:

    def __init__(self, side):
        self.side = side
        self.pairs = side // 2
        self.pitch = side + 2
        self.rows = BANK // side
        self.tiles = self.pairs // self.rows


FULL, HALF, QUART = Level(H0), Level(H0 // 2), Level(H0 // 4)

LAYERS = [("e0b0c1", 16), ("e0b0c2", 16), ("e0b1c1", 16), ("e0b1c2", 16), ("e1b0c1", 4), ("e1b0c2", 4), ("e1b1c1", 4),
          ("e1b1c2", 4), ("e2b0c1", 1), ("e2b0c2", 1), ("e2b1c1", 1), ("e2b1c2", 1), ("dec0", 4), ("dec1", 16), ("off", 16)]
PE_AT, PE_TILES = {}, 0
for _n, _t in LAYERS:
    PE_AT[_n] = PE_TILES
    PE_TILES += _t
DVE_AT, DVE_TILES = {}, 0
for _n, _t in [("norm1", 17), ("e0b0c2", 16), ("e0b1c2", 16), ("e1b1c2", 4), ("e2b1c2", 1), ("dec0", 4), ("dec1", 16),
               ("norm2", 17)]:
    DVE_AT[_n] = DVE_TILES
    DVE_TILES += _t
ACT_AT, ACT_TILES = {}, 0
for _n, _t in [("e0b0c1", 16), ("e0b1c1", 16), ("e1b0c1", 4), ("e1b0c2", 4), ("e1b1c1", 4), ("e2b0c1", 1), ("e2b0c2", 1),
               ("e2b1c1", 1), ("dec0", 4), ("dec1", 16), ("off", 16)]:
    ACT_AT[_n] = ACT_TILES
    ACT_TILES += _t


def loop(eng, start, end):
    if end - start == 1:
        yield start
    elif end > start:
        with eng.Fori(start, end) as i:
            yield i


def build(nc, x, w1, w2, wds, wdec, woff, boff, wdef, gmat, ident, sel, rampc, selg, places, out):
    es = ExitStack()
    with es:
        E = es.enter_context
        at = 0

        def place(name, shape, dt, offset):
            return nc.alloc_sbuf_tensor_at(name, shape, dt, offset=offset)

        def size(shape, dt):
            n = 4 if dt in (F32, I32) else 2
            for s in shape[1:]:
                n *= s
            return (n + 31) // 32 * 32

        class Map:

            def __init__(self, start):
                self.at = start

            def __call__(self, name, shape, dt=F32):
                t = place(name, shape, dt, self.at)
                self.at += size(shape, dt)
                assert self.at <= LIMIT, (name, self.at)
                return t

        LIMIT = nc.sbuf_usable_end

        base = (nc.sbuf_base + 31) // 32 * 32
        arena = E(nc.sbuf_tensor("arena", [P, (LIMIT - base) // 4 - 8], F32))

        m = Map(base)
        excess = m("excess", [50, IMAGES, 16])
        far = m("far", [50, 2])
        flag = m("flag", [1, 1], I32)
        maps_start = m.at
        xm, xc = m("xm", [P, 64, 130]), m("xc", [P, 66, 130])
        t_start = m.at
        tm, tc = m("tm", [P, 64, 130]), m("tc", [P, 66, 130])
        h = Map(t_start)
        hxm, hxc = h("hxm", [P, 32, 66]), h("hxc", [P, 34, 66])
        htm, htc = h("htm", [P, 32, 66]), h("htc", [P, 34, 66])
        qxm, qxc = h("qxm", [P, 16, 34]), h("qxc", [P, 18, 34])
        qtm, qtc = h("qtm", [P, 16, 34]), h("qtc", [P, 18, 34])
        work_end = m.at
        w1s = m("w1s", [P, len(CONV1), 6, 128])
        w2s = m("w2s", [P, 2, 6, 192])
        wdss = m("wdss", [P, 2, 192])
        wdecs = m("wdecs", [P, 2, 4, 128])
        woffs = m("woffs", [P, 6, 50])
        split = Map(m.at)
        raw = m("raw", [P, 2, 16, 128])
        turn = Map(m.at)
        tmp = m("tmp", [P, 4, BANK])
        turn_in = turn("turn_in", [P, 2, BANK])
        turned = turn("turned", [P, 2, BANK])
        off32 = split("off32", [50, 2, BANK])
        offr = split("offr", [50, 2, BANK])
        offp = split("offp", [50, 2, PARTS, BANK], BF16)
        offa = m("offa", [50, BANK])
        boffs = m("boffs", [50, 2])
        gmats = m("gmats", [P, 128])
        idents = m("idents", [P, 128])
        stats = m("stats", [P, 16, 6])
        mv = m("mv", [P, 2])
        gn = m("gn", [P, 12])
        zeros = m("zeros", [P, 256])

        m2 = Map(maps_start)
        sels = m2("sels", [P, 2 * TAPS, P], BF16)
        wdefs = m2("wdefs", [P, TAPS, P])
        offs = m2("offs", [P, 2, IMAGES, 2, BANK], BF16)
        win = m2("win", [P, 2, IMAGES, PATCHES, CH])
        dist = m2("dist", [P, DIST_RING, 2, BANK])
        hat = m2("hat", [P, 2, IMAGES, TAPS, BANK])
        val = m2("val", [P, 2, TAPS, PATCHES, PS * PS])
        x1t = m2("x1t", [P, 2, BANK])
        outt = m2("outt", [P, 2, BANK])

        m3 = Map(maps_start)
        g_sel = m3("g_sel", [BC_K, 2 * TAPS, P], BF16)
        g_wdef = m3("g_wdef", [CH, TAPS, CH])
        g_zero = m3("g_zero", [P, CH])
        g_nought = m3("g_nought", [P, BANK])
        g_offs = m3("g_offs", [BC_K, BANK], BF16)
        g_rows = m3("g_rows", [P, YSTEP, CH])
        g_hat_x = m3("g_hat_x", [P, BANK])
        g_y = m3("g_y", [P, BANK])
        g_t = m3("g_t", [P, YSTEP, BANK])
        g_hat = m3("g_hat", [P, YSTEP, BANK])
        g_val = m3("g_val", [CH, BANK])
        g_x1 = m3("g_x1", [CH, BANK])
        g_out = m3("g_out", [CH, BANK])

        X, T = (FULL, xm, xc), (FULL, tm, tc)
        HX, HT = (HALF, hxm, hxc), (HALF, htm, htc)
        QX, QT = (QUART, qxm, qxc), (QUART, qtm, qtc)

        psum = E(nc.psum_tensor("psum", [P, 8, BANK], F32))
        TURN_BANK, STAT_BANK = RING, RING + 2

        def sem(name):
            return E(nc.semaphore(name))

        w_in = sem("w_in")
        w_zero = sem("w_zero")
        c_in = sem("c_in")
        x_in = [sem(f"x_in{q}") for q in range(4)]
        raw_in = [sem(f"raw_in{q}") for q in range(2)]
        x1_out = sem("x1_out")
        pe_tiles = sem("pe_tiles")
        act_tiles = sem("act_tiles")
        dve_tiles = sem("dve_tiles")
        dve_step = sem("dve_step")
        stat_cols = sem("stat_cols")
        stat_sum = sem("stat_sum")
        var_ready = sem("var_ready")
        root_ready = sem("root_ready")
        cross_made = sem("cross_made")
        stats_in = sem("stats_in")
        final_rows = sem("final_rows")
        borders = sem("borders")
        turn_copied = sem("turn_copied")
        turn_done = sem("turn_done")
        turn_taken = sem("turn_taken")
        pm_out = [sem(f"pm_out{i}") for i in range(2)]
        off_ready = sem("off_ready")
        pool_step = sem("pool_step")
        off_split = sem("off_split")
        parts_out = [sem(f"parts_out{i}") for i in range(2)]

        sel_in = sem("sel_in")
        offs_in = [sem(f"offs_in{i}") for i in range(2)]
        win_in = [sem(f"win_in{i}") for i in range(2)]
        x1_in = [sem(f"x1_in{i}") for i in range(2)]
        dist_made = sem("dist_made")
        dist_abs = sem("dist_abs")
        hats_made = sem("hats_made")
        prod_pool = sem("prod_pool")
        prod_dve = sem("prod_dve")
        vals_made = sem("vals_made")
        vals_taken = sem("vals_taken")
        strip_conv = sem("strip_conv")
        strip_sum = sem("strip_sum")
        out_done = [sem(f"out_done{i}") for i in range(2)]

        excess_done = sem("excess_done")
        carried = sem("carried")
        zeros_set = sem("zeros_set")
        far_sum = sem("far_sum")
        far_sum_step = sem("far_sum_step")
        far_total = sem("far_total")
        flag_set = sem("flag_set")
        g_const = sem("g_const")
        g_offs_in = sem("g_offs_in")
        g_x1_in = sem("g_x1_in")
        g_rows_in = sem("g_rows_in")
        g_dist = sem("g_dist")
        g_abs = sem("g_abs")
        g_step = sem("g_step")
        g_hats = sem("g_hats")
        g_sampled = sem("g_sampled")
        g_taken = sem("g_taken")
        g_conv = sem("g_conv")
        g_sum = sem("g_sum")
        g_stored = sem("g_stored")

        MARGIN_SEMS = [x1_out, *pm_out, *out_done, g_stored]
        MARGIN, ONE = 16, 1
        ONE_SEMS = [final_rows, g_hats, g_conv, g_sampled, g_abs, g_sum, g_taken]

        x1d = nc.dram_tensor("x1d", [IMAGES, CH, H0, W0], F32, kind="Internal").ap()
        pixd = nc.dram_tensor("pixd", [IMAGES, PADH, PADW, CH], F32, kind="Internal").ap()
        offd = nc.dram_tensor("offd", [IMAGES, 16, OFFC, PARTS, 2, BANK], BF16, kind="Internal").ap()

        RELU, IDENT = ACT.Relu, ACT.Identity
        rows_of = lambda t, par: t[:, par::2, :]

        def bank(b):
            return psum[:, b, :]

        def by_rows(ap, level):
            return ap.rearrange("p (r w) -> p r w", w=level.side)

        def margins(eng, counted):
            n = 0
            for b in range(IMAGES):
                for at_ in (0, HALO + H0):
                    above = pixd[b, at_:at_ + HALO].rearrange("r w c -> (r w c)").rearrange("(p f) -> p f", p=P)
                    beside = pixd[b, HALO:HALO + H0, at_:at_ + HALO, :].rearrange("r w c -> r (w c)")
                    for dst in (above, beside):
                        if (MARGIN_SEMS + list(parts_out))[n] in counted:
                            eng.dma_start(dst, zeros[:, 0:dst.shape[1]]).then_inc((MARGIN_SEMS + list(parts_out))[n], MARGIN)
                        n += 1

        def settled(eng):
            eng.sem_inc(carried, 1)

        def general(eng, unit, end=None):
            eng.wait_ge(flag_set, 1)
            wanted = eng.value_load(flag[0:1, 0:1], min_val=0, max_val=1)
            with eng.If(wanted > 0):
                with eng.Fori(0, IMAGES) as b:
                    with eng.Fori(0, TILES8) as t:
                        for opar in range(2):
                            unit(b, t, opar, b * (2 * TILES8) + (2 * t + opar))
                if end is not None:
                    end()

        def dist_at(s, n):
            return dist[:, n % DIST_RING]

        assert UNITS % DIST_RING == 0

        block = E(nc.Block())

        @block.sync
        def _(sp):
            def load_x(b):
                sp.wait_ge(dve_tiles, b * DVE_TILES + RING)
                sp.wait_ge(x1_out, MARGIN + (b * 8 * 16))
                for q in range(4):
                    for par in range(2):
                        src = x[bass.ds(b, 1), :, 32 * q + par:32 * q + 32:2, :].rearrange("b c r w -> (b c) r w")
                        sp.dma_start(xm[64 * par:64 * par + 64, 16 * q:16 * q + 16, 1:129], src).then_inc(x_in[q], 16)

            def raw_rows(b, q):
                if q >= 2:
                    sp.wait_ge(final_rows, ONE + (b * 4 + q - 1))
                else:
                    sp.wait_ge(final_rows, ONE + (b * 4))
                    sp.wait_ge(off_split, b * 16 + 2)
                    settled(sp)
                    for s in range(2):
                        sp.wait_ge(parts_out[s], MARGIN + (b * 256))
                for par in range(2):
                    src = x[bass.ds(b, 1), :, 32 * q + par:32 * q + 32:2, :].rearrange("b c r w -> (b c) r w")
                    sp.dma_start(raw[64 * par:64 * par + 64, q % 2], src).then_inc(raw_in[q % 2], 16)

            def x1_rows(b, q):
                sp.wait_ge(final_rows, ONE + (b * 4 + q + 1))
                for par in range(2):
                    dst = x1d[bass.ds(b, 1), :, 32 * q + par:32 * q + 32:2, :].rearrange("b c r w -> (b c) r w")
                    sp.dma_start(dst, xm[64 * par:64 * par + 64, 16 * q:16 * q + 16, 1:129]).then_inc(x1_out, 16)

            for counted in ONE_SEMS:
                sp.sem_inc(counted, ONE)
            sp.dma_start(gmats[:], gmat).then_inc(c_in, 16)
            sp.dma_start(idents[:], ident).then_inc(c_in, 16)
            sp.dma_start(boffs[:], boff).then_inc(c_in, 16)
            with sp.Fori(0, IMAGES) as b:
                load_x(b)
                raw_rows(b, 0)
                raw_rows(b, 1)
                for q in range(4):
                    x1_rows(b, q)
                    if q + 2 < 4:
                        raw_rows(b, q + 2)
            sp.wait_ge(x1_out, MARGIN + (IMAGES * 8 * 16))
            for i in range(2):
                sp.wait_ge(pm_out[i], MARGIN + (IMAGES * 8 * 16))
                sp.wait_ge(parts_out[i], MARGIN + (IMAGES * 8 * 32))
            for margin in MARGIN_SEMS[3:]:
                sp.wait_ge(margin, MARGIN)
            sp.wait_ge(act_tiles, IMAGES * ACT_TILES + RING)
            sp.wait_ge(dve_tiles, IMAGES * DVE_TILES + RING)
            sp.wait_ge(pe_tiles, IMAGES * PE_TILES)
            sp.wait_ge(turn_done, IMAGES * 16 + 2)
            sp.wait_ge(off_split, IMAGES * 16 + 2)

            def load_offs(t, slot):
                for b in range(IMAGES):
                    src = offd[b, bass.ds(t, 1)].rearrange("t c p w n -> (t c p) (w n)")
                    sp.dma_start(offs[0:BC_K - 3, slot, b].rearrange("c w n -> c (w n)"), src).then_inc(offs_in[slot], 16)

            def load_windows(t, j):
                for b in range(IMAGES):
                    for wr in range(WIN):
                        src = pixd[b, bass.ds(2 * PS * t + (PS * j + wr), 1)]
                        src = bass.AP(src.tensor, src.offset, [[CH, WIN], [PS * CH, PATCHES], [1, CH]])
                        sp.dma_start(win[WIN * wr:WIN * wr + WIN, j, b], src).then_inc(win_in[j], 16)

            def load_x1(t, j):
                src = x1d[:, :, bass.ds(2 * PS * t + PS * j, PS), :].rearrange("b c r w -> (b c) (r w)")
                sp.dma_start(x1t[:, j, :], src).then_inc(x1_in[j], 16)

            def store_strip(t, j):
                sp.wait_ge(strip_sum, 2 * t + (j + 1))
                dst = out[:, :, bass.ds(2 * PS * t + PS * j, PS), :].rearrange("b c r w -> (b c) (r w)")
                sp.dma_start(dst, outt[:, j, :]).then_inc(out_done[j], 16)

            sp.dma_start(sels[:], sel).then_inc(sel_in, 16)
            for slot in range(2):
                for b in range(IMAGES):
                    sp.dma_start(offs[BC_K - 3:P, slot, b].rearrange("c w n -> c (w n)"), rampc).then_inc(sel_in, 16)
            sp.dma_start(wdefs[:], wdef).then_inc(sel_in, 16)
            nought = pixd[0, 0:HALO]
            n = IMAGES * PATCHES * CH
            assert n <= HALO * PADW * CH
            for j in range(2):
                sp.dma_start(win[WPX:P, j].rearrange("p b q c -> p (b q c)"),
                             bass.AP(nought.tensor, nought.offset, [[0, P - WPX], [1, n]])).then_inc(sel_in, 16)
            load_offs(0, 0)
            for j in range(2):
                load_windows(0, j)
                load_x1(0, j)
            load_offs(1, 1)

            def strip_pair(t, slot, more):
                for j in range(2):
                    if more:
                        sp.wait_ge(vals_made, GROUPS * (2 * t + (j + 1)))
                        load_windows(t + 1, j)
                    store_strip(t, j)
                    if more:
                        load_x1(t + 1, j)
                if more == 2:
                    load_offs(t + 2, slot)

            with sp.Fori(0, STRIPS // 4 - 1) as h:
                strip_pair(2 * h, 0, 2)
                strip_pair(2 * h + 1, 1, 2)
            strip_pair(STRIPS // 2 - 2, 0, 1)
            strip_pair(STRIPS // 2 - 1, 1, 0)
            for j in range(2):
                sp.wait_ge(out_done[j], MARGIN + (16 * (STRIPS // 2)))

            def g_unit(b, t, opar, u):
                sp.wait_ge(g_stored, MARGIN + (16 * u))
                src = offd[bass.ds(b, 1), bass.ds(t, 1), :, :, opar].rearrange("b t c p n -> (b t c p) n")
                sp.dma_start(g_offs[0:BC_K - 3], src).then_inc(g_offs_in, 16)
                sp.dma_start(g_offs[BC_K - 3:BC_K], places[bass.ds(t, 1), opar].rearrange("t r n -> (t r) n")
                             ).then_inc(g_offs_in, 16)
                rows = lambda d: d[bass.ds(b, 1), :, bass.ds(8 * t, 8), :].rearrange("b c (i two) w -> two (b c) i w", two=2)[opar]
                sp.dma_start(g_x1[:].rearrange("c (i w) -> c i w", w=W0), rows(x1d)).then_inc(g_x1_in, 16)
                with sp.Fori(0, TAPS) as k:
                    with sp.Fori(0, CHUNKS) as y:
                        n = u * (TAPS * CHUNKS) + (k * CHUNKS + y)
                        sp.wait_ge(g_sampled, ONE + (n))
                        src = pixd[bass.ds(b, 1), bass.ds(YSTEP * y + HALO, YSTEP), HALO:HALO + W0, :]
                        sp.dma_start(g_rows[:], src.rearrange("b r w c -> w (b r) c")).then_inc(g_rows_in, 16)
                sp.wait_ge(g_sum, ONE + (u + 1))
                sp.dma_start(rows(out), g_out[:].rearrange("c (i w) -> c i w", w=W0)).then_inc(g_stored, 16)

            sp.wait_ge(strip_sum, STRIPS)
            sp.dma_start(g_sel[:], selg).then_inc(g_const, 16)
            sp.dma_start(g_wdef[:], wdef[0:CH, :, 0:CH]).then_inc(g_const, 16)
            def g_end():
                sp.wait_ge(g_stored, MARGIN + 16 * 2 * TILES8 * IMAGES)

            general(sp, g_unit, g_end)
            sp.wait_ge(g_const, 48)

        @block.tensor
        def _(pe):
            def after(sem_, per_image, b, n):
                pe.wait_ge(sem_, b * per_image + (n + RING))

            def own_and_prev(b, layer, prev, it, u, tiles):
                psem, pper, ptot, pT = prev
                t0 = PE_AT[layer]
                if u == 0:
                    after(psem, pper, b, ptot - 1 if pT > 2 and tiles > 1 else ptot)
                if u == 1:
                    after(psem, pper, b, ptot)
                sem_, per, base_ = (act_tiles, ACT_TILES, ACT_AT[layer]) if layer in ACT_AT else \
                    (dve_tiles, DVE_TILES, DVE_AT[layer])
                pe.wait_ge(sem_, b * per + (4 * it + (base_ + u + 1)))

            def conv3(b, layer, src, mats, prev, extra=None):
                L, M, C = src
                n = L.rows
                T_ = L.tiles
                for it in loop(pe, 0, max(T_ // 4, 1)):
                    for u in range(min(T_, 4)):
                        own_and_prev(b, layer, prev, it, u, T_)
                        i0 = (4 * it + u) * n
                        o = by_rows(bank((PE_AT[layer] + u) % RING), L)
                        todo = [(mats(kx), M[:, bass.ds(i0, n), kx:kx + L.side]) for kx in range(3)]
                        todo += [(mats(CROSS + kx), C[:, bass.ds(i0 + 1, n), kx:kx + L.side]) for kx in range(3)]
                        if extra:
                            todo += extra(i0, n)
                        emit(o, todo)

            def emit(o, todo):
                for j, (w, rows) in enumerate(todo):
                    mm = pe.matmul(o, w, rows, start=j == 0, stop=j == len(todo) - 1)
                mm.then_inc(pe_tiles, 1)

            def halves(src, opar, j0, n, taps, Ld):
                return src.rearrange("p (j two) w -> p j two w", two=2)[:, bass.ds(j0, n), opar, taps:taps + 2 * Ld.side:2]

            def conv3_s2(b, layer, src, dst, which, prev):
                L, M, C = src
                D = dst[0]
                n = D.rows
                cross = C[:, 1:1 + L.pairs, :]
                for it in loop(pe, 0, max(D.tiles // 4, 1)):
                    for u in range(min(D.tiles, 4)):
                        own_and_prev(b, layer, prev, it, u, D.tiles)
                        j0 = (4 * it + u) * n
                        o = by_rows(bank((PE_AT[layer] + u) % RING), D)
                        todo = []
                        for opar in range(2):
                            lo = 64 - 64 * opar
                            for kx in range(3):
                                todo.append((w2s[:, which, kx, lo:lo + 128], halves(M, opar, j0, n, kx, D)))
                                todo.append((w2s[:, which, CROSS + kx, lo:lo + 128], halves(cross, opar, j0, n, kx, D)))
                        emit(o, todo)

            def ds_terms(src, which, D):
                def terms(j0, n):
                    return [(wdss[:, which, 64 - 64 * opar:192 - 64 * opar], halves(src[1], opar, j0, n, 1, D))
                            for opar in range(2)]
                return terms

            def deconv(b, layer, src, which, prev):
                L, M, _ = src
                for it in loop(pe, 0, L.tiles):
                    for u in range(4):
                        own_and_prev(b, layer, prev, it, u, 4)
                        o = by_rows(bank((PE_AT[layer] + u) % RING), L)
                        emit(o, [(wdecs[:, which, u, :], M[:, bass.ds(it * L.rows, L.rows), 1:1 + L.side])])

            def group_sums(n):
                for j in range(2):
                    pe.wait_ge(stat_cols, 2 * n + (j + 1))
                    pe.matmul(psum[:, STAT_BANK, j:j + 1], gmats[:], gn[:, 4 * j:4 * j + 1],
                              start=True, stop=True).then_inc(stat_sum, 1)

            def prev_of(layer, T_):
                if layer in DVE_AT:
                    return (dve_tiles, DVE_TILES, DVE_AT[layer] + T_, T_)
                return (act_tiles, ACT_TILES, ACT_AT[layer] + T_, T_)

            def w_of(n):
                return lambda j: w1s[:, n, j, :]

            pe.nop().then_inc(turn_done, 2)
            pe.wait_ge(c_in, 3 * 16)
            with pe.Fori(0, IMAGES) as b:
                group_sums(2 * b)
                pe.wait_ge(w_in, W_DMAS * 16)
                for it in loop(pe, 0, 4):
                    for u in range(4):
                        after(dve_tiles, DVE_TILES, b, 4 * it + (u + 2))
                        pe.wait_ge(act_tiles, b * ACT_TILES + (4 * it + (u + 1)))
                        i0 = (4 * it + u) * 4
                        todo = [(w1s[:, 0, kx, :], xm[:, bass.ds(i0, 4), kx:kx + 128]) for kx in range(3)]
                        todo += [(w1s[:, 0, CROSS + kx, :], xc[:, bass.ds(i0 + 1, 4), kx:kx + 128]) for kx in range(3)]
                        emit(by_rows(bank(u), FULL), todo)
                conv3(b, "e0b0c2", T, w_of(1), prev_of("e0b0c1", 16))
                conv3(b, "e0b1c1", X, w_of(2), prev_of("e0b0c2", 16))
                conv3(b, "e0b1c2", T, w_of(3), prev_of("e0b1c1", 16))
                conv3_s2(b, "e1b0c1", X, HT, 0, prev_of("e0b1c2", 16))
                conv3(b, "e1b0c2", HT, w_of(4), prev_of("e1b0c1", 4), ds_terms(X, 0, HALF))
                conv3(b, "e1b1c1", HX, w_of(5), prev_of("e1b0c2", 4))
                conv3(b, "e1b1c2", HT, w_of(6), prev_of("e1b1c1", 4))
                conv3_s2(b, "e2b0c1", HX, QT, 1, prev_of("e1b1c2", 4))
                conv3(b, "e2b0c2", QT, w_of(7), prev_of("e2b0c1", 1), ds_terms(HX, 1, QUART))
                conv3(b, "e2b1c1", QX, w_of(8), prev_of("e2b0c2", 1))
                conv3(b, "e2b1c2", QT, w_of(9), prev_of("e2b1c1", 1))
                deconv(b, "dec0", QX, 0, prev_of("e2b1c2", 1))
                deconv(b, "dec1", HX, 1, prev_of("dec0", 4)[:3] + (1,))
                group_sums(2 * b + 1)
                for it in loop(pe, 0, 4):
                    for u in range(4):
                        after(dve_tiles, DVE_TILES, b, 4 * it + (DVE_AT["norm2"] + u + 2))
                        pe.wait_ge(act_tiles, b * ACT_TILES + (4 * it + (ACT_AT["off"] + u + 1)))
                        i0 = (4 * it + u) * 4
                        o = psum[0:50, u, :].rearrange("p (r w) -> p r w", w=128)
                        todo = [(woffs[:, kx, :], tm[:, bass.ds(i0, 4), kx:kx + 128]) for kx in range(3)]
                        todo += [(woffs[:, CROSS + kx, :], tc[:, bass.ds(i0 + 1, 4), kx:kx + 128]) for kx in range(3)]
                        emit(o, todo)
                        s = u % 2
                        pe.wait_ge(turn_copied, b * 16 + (4 * it + (u + 1)))
                        pe.wait_ge(turn_taken, b * 16 + (4 * it + (u + 1)))
                        for r in range(4):
                            mm = pe.transpose(psum[:, TURN_BANK + s, 128 * r:128 * r + 128],
                                              turn_in[:, s, 128 * r:128 * r + 128], idents[:])
                        mm.then_inc(turn_done, 1)

            def distances(s, s_of, n):
                t, j = s_of
                b, k = divmod(n, TAPS)
                if n == 0:
                    pe.wait_ge(offs_in[t[1]], t[2])
                if isinstance(s, int) and s == 0 and n < 2:
                    pass
                else:
                    pe.wait_ge(dist_abs, UNITS * s + (n - 1))
                slot = n % 2
                rows = offs[:, t[1], b, :, (BANK // 2) * j:(BANK // 2) * (j + 1)]
                for axis in range(2):
                    mm = pe.matmul(psum[:, 2 * slot + axis, :].rearrange("p (w n) -> p w n", w=2),
                                   sels[:, 2 * k + axis, :], rows, start=True, stop=True)
                mm.then_inc(dist_made, 1)

            def sample_group(s, j, g):
                if g == 0:
                    pe.wait_ge(win_in[j[0]], j[1])
                    pe.wait_ge(prod_pool, len(POOL_UNITS) * (s + 1))
                    pe.wait_ge(prod_dve, len(DVE_UNITS) * (s + 1))
                if g >= 3:
                    pe.wait_ge(vals_taken, GROUPS * s + (g - 2))
                elif not (isinstance(s, int) and s == 0):
                    pe.wait_ge(vals_taken, GROUPS * (s - 1) + (GROUPS - (GROUPS - 1 - g) % 3))
                o = psum[:, VAL_BANKS[g % 3], :]
                last = min(PATCHES, GROUP * (g + 1))
                for q, p in enumerate(range(GROUP * g, last)):
                    w = TAPS * PS * PS
                    for b in range(IMAGES):
                        dst = o[CH * b:CH * b + CH, w * q:w * q + w].rearrange("c (k r x) -> c k r x", k=TAPS, x=PS)
                        mm = pe.matmul(dst, win[:, j[0], b, p, :],
                                       hat[:, j[0], b].rearrange("p k (r x) -> p k r x", r=PS)[:, :, :, PS * p:PS * p + PS],
                                       start=True, stop=True, skip_group_check=True)
                mm.then_inc(vals_made, 1)

            def weigh(s, j, ks):
                if ks[0] == 0:
                    pe.wait_ge(vals_taken, GROUPS * (s + 1))
                    if not (isinstance(s, int) and s == 0):
                        pe.wait_ge(strip_sum, s)
                        settled(pe)
                for k in ks:
                    mm = pe.matmul(psum[:, SUM_BANK, :].rearrange("c (r p x) -> c r p x", r=PS, x=PS), wdefs[:, k, :],
                                   val[:, j, k].rearrange("c p (r x) -> c r p x", r=PS), start=k == 0, stop=k == TAPS - 1)
                if ks[-1] == TAPS - 1:
                    mm.then_inc(strip_conv, 1)

            def strip_step(s, j, t_next, s_next):
                for n in range(UNITS):
                    if s_next is not None:
                        distances(s_next, t_next, n)
                    for g in range(GROUPS):
                        if g * UNITS // GROUPS == n:
                            sample_group(s, j, g)
                    if 3 <= n < 3 + TAPS and not (isinstance(s, int) and s == 0):
                        weigh(s - 1, 1 - j[0], range(n - 3, n - 2))

            def quad(h, first=False, last=False):
                for r in range(4):
                    s, j = 4 * h + r, r % 2
                    win_count = (2 * h + r // 2 + 1) * (16 * WIN * IMAGES)
                    s_next, jn = s + 1, (r + 1) % 2
                    slot = ((r + 1) // 2) % 2
                    count = (h + (1 if r < 3 else 2)) * (16 * IMAGES)
                    t_next = ((None, slot, count), jn)
                    end = last and r == 3
                    strip_step(s, (j, win_count), t_next, None if end else s_next)

            pe.wait_ge(far_sum, 1)
            pe.matmul(psum[0:1, STAT_BANK, 0:1], far[:, 0:1], far[:, 1:2], start=True, stop=True).then_inc(far_total, 1)
            pe.wait_ge(flag_set, 1)
            pe.wait_ge(sel_in, 16 * (1 + 2 * IMAGES + 1 + 2))
            for n in range(UNITS):
                distances(0, ((None, 0, 16 * IMAGES), 0), n)
            quad(0)
            with pe.Fori(1, STRIPS // 4 - 1) as h:
                quad(h)
            quad(STRIPS // 4 - 1, last=True)
            weigh(STRIPS - 1, 1, range(TAPS))

            def g_unit(b, t, opar, u):
                pe.wait_ge(g_offs_in, u * 32 + 32)
                for k in range(TAPS):
                    tap = u * TAPS + k
                    pe.wait_ge(g_abs, ONE + (2 * tap))
                    for axis in range(2):
                        mm = pe.matmul(psum[:, axis, :], g_sel[:, 2 * k + axis, :], g_offs[:], start=True, stop=True)
                    mm.then_inc(g_dist, 1)
                    pe.wait_ge(g_taken, ONE + (tap))
                    acc = psum[0:CH, 2, :]
                    pe.matmul(acc, g_zero[:], g_nought[:], start=True, stop=False, skip_group_check=True)
                    with pe.Fori(0, CHUNKS) as y:
                        n = tap * CHUNKS + y
                        pe.wait_ge(g_rows_in, 16 * n + 16)
                        pe.wait_ge(g_hats, ONE + (n + 1))
                        for r in range(YSTEP):
                            mm = pe.matmul(acc, g_rows[:, r, :], g_hat[:, r, :], start=False, stop=False,
                                           skip_group_check=True)
                        mm.then_inc(g_sampled, 1)
                    pe.wait_ge(g_taken, ONE + (tap + 1))
                    if k == 0:
                        pe.wait_ge(g_sum, ONE + (u))
                    settled(pe)
                    pe.matmul(psum[0:CH, 3, :], g_wdef[:, k, :], g_val[:], start=k == 0, stop=k == TAPS - 1,
                              skip_group_check=True).then_inc(g_conv, 1)

            
            pe.wait_ge(g_const, 48)
            general(pe, g_unit)

        @block.scalar
        def _(act):
            def blocks(tile_, src, cols, width):
                for par in range(2):
                    for opar in range(2):
                        act.dma_start(tile_(64 * par, 0, cols * opar, width), src(par - opar + 1)).then_inc(w_in, 16)
                act.dma_start(tile_(0, CROSS, cols, width), src(2)).then_inc(w_in, 16)
                act.dma_start(tile_(64, CROSS, 0, width), src(0)).then_inc(w_in, 16)

            def load_weights():
                act.wait_ge(w_zero, 1)
                for conv in range(len(CONV1)):
                    blocks(lambda p, j, c, n: w1s[p:p + 64, conv, j:j + 3, c:c + n], lambda ky: w1[:, conv, ky], 64, 64)
                for which in range(2):
                    for par in range(2):
                        rows = slice(64 * par, 64 * par + 64)
                        act.dma_start(w2s[rows, which, 0:3, 64:128], w2[:, which, 1 + par]).then_inc(w_in, 16)
                        act.dma_start(wdecs[rows, which, 2 * par:2 * par + 2, :], wdec[:, which]).then_inc(w_in, 16)
                    act.dma_start(w2s[64:128, which, CROSS:CROSS + 3, 64:128], w2[:, which, 0]).then_inc(w_in, 16)
                act.dma_start(wdss[0:64, :, 64:128], wds).then_inc(w_in, 16)
                blocks(lambda p, j, c, n: woffs[p:p + 64, j:j + 3, c:c + n], lambda ky: woff[:, ky], ODD_AT, OFFC)
                act.wait_ge(zeros_set, 1)
                margins(act, MARGIN_SEMS)

            def relu_rows(b, layer, dst):
                L, M, C = dst
                n = L.rows
                for it in loop(act, 0, max(L.tiles // 4, 1)):
                    for u in range(min(L.tiles, 4)):
                        act.wait_ge(pe_tiles, b * PE_TILES + (4 * it + (PE_AT[layer] + u + 1)))
                        i0 = (4 * it + u) * n
                        src = by_rows(bank((PE_AT[layer] + u) % RING), L)
                        inner = slice(1, 1 + L.side)
                        act.activation(M[:, bass.ds(i0, n), inner], src, RELU, scale=BN_S)
                        act.activation(C[0:64, bass.ds(i0, n), inner], src[0:64], RELU, scale=BN_S)
                        act.activation(C[64:128, bass.ds(i0 + 2, n), inner], src[64:128], RELU,
                                       scale=BN_S).then_inc(act_tiles, 1)

            def relu_tmp(b, layer, L):
                for it in loop(act, 0, L.tiles):
                    for u in range(4):
                        act.wait_ge(pe_tiles, b * PE_TILES + (4 * it + (PE_AT[layer] + u + 1)))
                        act.wait_ge(dve_tiles, b * DVE_TILES + (4 * it + (DVE_AT[layer] + u + 1)))
                        act.activation(tmp[:, u, :], bank((PE_AT[layer] + u) % RING), RELU,
                                       scale=BN_S).then_inc(act_tiles, 1)

            def root(n):
                act.wait_ge(var_ready, n + 1)
                act.activation(gn[:, 6:7], gn[:, 5:6], ACT.Sqrt).then_inc(root_ready, 1)

            load_weights()
            act.nop().then_inc(act_tiles, RING)
            act.nop().then_inc(turn_taken, 2)
            act.wait_ge(c_in, 3 * 16)
            with act.Fori(0, IMAGES) as b:
                root(2 * b)
                act.wait_ge(borders, b * 2 + 1)
                relu_rows(b, "e0b0c1", T)
                relu_rows(b, "e0b1c1", T)
                act.wait_ge(borders, b * 2 + 2)
                relu_rows(b, "e1b0c1", HT)
                relu_rows(b, "e1b0c2", HX)
                relu_rows(b, "e1b1c1", HT)
                relu_rows(b, "e2b0c1", QT)
                relu_rows(b, "e2b0c2", QX)
                relu_rows(b, "e2b1c1", QT)
                for s in range(2):
                    act.wait_ge(pm_out[s], MARGIN + (b * 128))
                relu_tmp(b, "dec0", QUART)
                relu_tmp(b, "dec1", HALF)
                root(2 * b + 1)
                for it in loop(act, 0, 4):
                    for u in range(4):
                        s, uses = u % 2, u // 2
                        act.wait_ge(pe_tiles, b * PE_TILES + (4 * it + (PE_AT["off"] + u + 1)))
                        act.wait_ge(off_split, b * 16 + (4 * it + (u + 1)))
                        act.wait_ge(parts_out[s], MARGIN + (b * 256 + (64 * it + 32 * uses)))
                        act.activation(off32[:, s, :], psum[0:50, u, :], IDENT, bias=boffs[:, 0:1])
                        act.activation(offp[:, s, 0, :], psum[0:50, u, :], IDENT,
                                       bias=boffs[:, 0:1])
                        act.activation(offa[:], psum[0:50, u, :], ACT.Abs, bias=boffs[:, 0:1]).then_inc(act_tiles, 1)
                        act.wait_ge(act_tiles, b * ACT_TILES + (4 * it + (RING + ACT_AT["off"] + u + 1)))
                        act.activation(offa[:], offa[:], RELU, bias=boffs[:, 1:2],
                                       accum_out=excess[:, bass.ds(b, 1), bass.ds(4 * it + u, 1)].rearrange("p b t -> p (b t)")).then_inc(excess_done, 1)
                        act.wait_ge(excess_done, b * 16 + (4 * it + (u + 1)))
                        act.wait_ge(turn_done, b * 16 + (4 * it + (u + 3)))
                        act.wait_ge(pm_out[s], MARGIN + (b * 128 + (32 * it + 16 * uses)))
                        act.activation(turned[:, s, :], psum[:, TURN_BANK + s, :], ACT.Copy).then_inc(turn_taken, 1)
                        act.wait_ge(turn_taken, b * 16 + (4 * it + (u + 3)))
                        dst = pixd[bass.ds(b, 1), bass.ds(32 * it + (8 * u + HALO), 8), HALO:HALO + W0, :]
                        act.dma_start(dst.rearrange("b r w c -> w (b r) c"),
                                      turned[:, s, :].rearrange("w (r c) -> w r c", c=CH)).then_inc(pm_out[s], 16)

            act.wait_ge(excess_done, 16 * IMAGES)
            act.nop().then_inc(act_tiles, 1)

            def strip_abs(s, first=False):
                for n in range(UNITS):
                    act.wait_ge(dist_made, UNITS * s + (n + 1))
                    if n >= DIST_RING or not first:
                        m_ = n - DIST_RING
                        q = s if m_ >= 0 else s - 1
                        m_ %= UNITS
                        who, mine = (prod_pool, POOL_UNITS) if m_ in POOL_UNITS else (prod_dve, DVE_UNITS)
                        act.wait_ge(who, len(mine) * q + (mine.index(m_) + 1))
                    slot = 2 * (n % 2)
                    act.activation(dist_at(s, n), psum[:, slot:slot + 2, :], ACT.Abs).then_inc(dist_abs, 1)

            strip_abs(0, True)
            strip_abs(1)
            with act.Fori(1, STRIPS // 2) as h:
                strip_abs(2 * h)
                strip_abs(2 * h + 1)

            def g_unit(b, t, opar, u):
                with act.Fori(0, TAPS) as k:
                    tap = u * TAPS + k
                    act.wait_ge(g_dist, tap + 1)
                    act.wait_ge(g_hats, ONE + (tap * CHUNKS))
                    act.activation(g_hat_x[:], psum[:, 0, :], ACT.Abs).then_inc(g_abs, 1)
                    act.activation(g_y[:], psum[:, 1, :], ACT.Copy).then_inc(g_abs, 1)

            general(act, g_unit)

        @block.vector
        def _(dve):
            def add_relu_rows(b, layer, dst, s0):
                L, M, C = dst
                n = L.rows
                for it in loop(dve, 0, max(L.tiles // 4, 1)):
                    for u in range(min(L.tiles, 4)):
                        dve.wait_ge(pe_tiles, b * PE_TILES + (4 * it + (PE_AT[layer] + u + 1)))
                        i0 = (4 * it + u) * n
                        src = by_rows(bank((PE_AT[layer] + u) % RING), L)
                        inner = slice(1, 1 + L.side)
                        rows = M[:, bass.ds(i0, n), inner]
                        dve.scalar_tensor_tensor(out=rows, in0=src, scalar=BN_S, in1=rows, op0=ALU.mult,
                                                 op1=ALU.add).then_inc(dve_step, 1)
                        dve.wait_ge(dve_step, b * STEPS + (4 * it + (s0 + u + 1)))
                        dve.tensor_scalar(C[0:64, bass.ds(i0, n), inner], M[0:64, bass.ds(i0, n), inner], 0.0, None, ALU.max)
                        dve.tensor_scalar(C[64:128, bass.ds(i0 + 2, n), inner], M[64:128, bass.ds(i0, n), inner], 0.0, None,
                                          ALU.max).then_inc(cross_made, 1)
                        dve.wait_ge(cross_made, b * CROSSES + (4 * it + (CROSS_AT[layer] + u + 1)))
                        dve.tensor_scalar(rows, rows, 0.0, None, ALU.max).then_inc(dve_tiles, 1)

            S_GN1, S_C2, S_C4, S_C8, S_C12, S_D0 = 0, 7, 23, 39, 43, 44
            S_D1 = S_D0 + 4
            S_GN2 = S_D1 + 16
            STEPS = S_GN2 + 7

            def group_stats(b, j, s0):
                def step(k):
                    dve.wait_ge(dve_step, b * STEPS + (s0 + k))

                dve.bn_aggr(mv[:], stats[:]).then_inc(dve_step, 1)
                step(1)
                dve.tensor_copy(gn[:, 0:1], mv[:, 0:1]).then_inc(stat_cols, 1)
                dve.wait_ge(stat_sum, 4 * b + (2 * j + 1))
                dve.tensor_copy(gn[:, 2:3], psum[:, STAT_BANK, 0:1]).then_inc(dve_step, 1)
                step(2)
                dve.tensor_tensor(gn[:, 1:2], mv[:, 0:1], gn[:, 2:3], ALU.subtract).then_inc(dve_step, 1)
                step(3)
                dve.scalar_tensor_tensor(out=gn[:, 4:5], in0=gn[:, 1:2], scalar=gn[:, 1:2], in1=mv[:, 1:2], op0=ALU.mult,
                                         op1=ALU.add).then_inc(stat_cols, 1)
                dve.wait_ge(stat_sum, 4 * b + (2 * j + 2))
                dve.tensor_scalar(gn[:, 5:6], psum[:, STAT_BANK, 1:2], GN_EPS, None, ALU.add).then_inc(var_ready, 1)
                dve.wait_ge(root_ready, 2 * b + (j + 1))
                dve.reciprocal(gn[:, 7:8], gn[:, 6:7]).then_inc(dve_step, 1)
                step(4)
                dve.scalar_tensor_tensor(out=gn[:, 8:9], in0=gn[:, 7:8], scalar=gn[:, 7:8], in1=gn[:, 5:6], op0=ALU.mult,
                                         op1=ALU.mult).then_inc(dve_step, 1)
                step(5)
                dve.tensor_scalar(gn[:, 8:9], gn[:, 8:9], -0.5, 1.5, ALU.mult, ALU.add).then_inc(dve_step, 1)
                step(6)
                dve.tensor_tensor(gn[:, 9:10], gn[:, 7:8], gn[:, 8:9], ALU.mult).then_inc(dve_step, 1)
                step(7)
                settled(dve)

            CROSS_AT = {"norm1": 0, "e0b0c2": 16, "e0b1c2": 32, "e1b1c2": 48, "e2b1c2": 52}
            CROSSES = 53

            def normalise(b, dst):
                L, M, C = dst

                def rows(it, last):
                    i0 = it * 4
                    inner = slice(1, 129)
                    for o, s in ((C[0:64, bass.ds(i0, 4), inner], slice(0, 64)),
                                 (C[64:128, bass.ds(i0 + 2, 4), inner], slice(64, 128)),
                                 (M[:, bass.ds(i0, 4), inner], slice(0, 128))):
                        if M is xm and s.stop - s.start == 128:
                            ins.then_inc(cross_made, 1)
                            dve.wait_ge(cross_made, b * CROSSES + it + 1)
                        ins = dve.tensor_scalar(o, xm[s, bass.ds(i0, 4), inner], gn[s, 2:3], gn[s, 9:10], ALU.subtract,
                                                ALU.mult)
                    ins.then_inc(dve_tiles, 2 if last else 1)

                with dve.Fori(0, 15) as it:
                    rows(it, False)
                rows(15, True)

            def dec0_rows(b):
                for u in range(4):
                    par, l = divmod(u, 2)
                    dve.wait_ge(act_tiles, b * ACT_TILES + (RING + ACT_AT["dec0"] + u + 1))
                    rows = hxm[:, par::2, 1 + l:1 + l + 64:2]
                    dve.tensor_tensor(rows, by_rows(tmp[:, u, :], QUART), rows, ALU.add).then_inc(dve_step, 1)
                    dve.wait_ge(dve_step, b * STEPS + (S_D0 + u + 1))
                    dve.tensor_scalar(rows, rows, BN_S, None, ALU.mult).then_inc(dve_tiles, 1)

            def dec1_rows(b):
                for it in loop(dve, 0, 2):
                    for half in range(2):
                        pairs = xm[:, bass.ds(32 * it + 16 * half, 16), :]
                        for u in range(4):
                            par, l = divmod(u, 2)
                            dve.wait_ge(act_tiles, b * ACT_TILES + (8 * it + (RING + ACT_AT["dec1"] + 4 * half + u + 1)))
                            rows = pairs[:, par::2, 1 + l:1 + l + 128:2]
                            dve.tensor_tensor(rows, by_rows(tmp[:, u, :], HALF), rows, ALU.add).then_inc(dve_tiles, 1)
                        dve.wait_ge(dve_tiles, b * DVE_TILES + (8 * it + (RING + DVE_AT["dec1"] + 4 * half + 4)))
                        dve.wait_ge(raw_in[half], b * 64 + (32 * it + 32))
                        for c in range(4):
                            rows = xm[:, bass.ds(32 * it + (16 * half + 4 * c), 4), 1:129]
                            ins = dve.scalar_tensor_tensor(out=rows, in0=rows, scalar=BN_S, in1=raw[:, half, 4 * c:4 * c + 4, :],
                                                           op0=ALU.mult, op1=ALU.add)
                            ins.then_inc(dve_step, 1)
                        for c in range(4):
                            rows = xm[:, bass.ds(32 * it + (16 * half + 4 * c), 4), 1:129]
                            dve.wait_ge(dve_step, b * STEPS + (8 * it + (S_D1 + 4 * half + c + 1)))
                            ins = dve.bn_stats(stats[:, bass.ds(8 * it + (4 * half + c), 1), :].rearrange("p a s -> p (a s)"), rows)
                        ins.then_inc(final_rows, 1)

            dve.memset(w1s[:], 0.0)
            dve.memset(w2s[:], 0.0)
            dve.memset(wdss[:], 0.0)
            dve.memset(wdecs[:], 0.0)
            dve.memset(woffs[:], 0.0)
            dve.memset(xm[:, :, 0:130:129], 0.0)
            dve.memset(xc[:, :, 0:130:129], 0.0)
            dve.memset(xc[:, 1:65:63, 1:129], 0.0).then_inc(w_zero, 1)
            dve.nop().then_inc(dve_tiles, RING)
            with dve.Fori(0, IMAGES) as b:
                for q in range(4):
                    dve.wait_ge(x_in[q], b * 32 + 32)
                    for c in range(4):
                        t = 4 * q + c
                        ins = dve.bn_stats(stats[:, t, :], xm[:, 4 * t:4 * t + 4, 1:129])
                ins.then_inc(stats_in, 1)
                dve.wait_ge(stats_in, b + 1)
                settled(dve)
                group_stats(b, 0, S_GN1)
                normalise(b, X)
                add_relu_rows(b, "e0b0c2", X, S_C2)
                add_relu_rows(b, "e0b1c2", X, S_C4)
                add_relu_rows(b, "e1b1c2", HX, S_C8)
                add_relu_rows(b, "e2b1c2", QX, S_C12)
                dec0_rows(b)
                dec1_rows(b)
                dve.wait_ge(final_rows, ONE + (4 * b + 4))
                settled(dve)
                group_stats(b, 1, S_GN2)
                dve.wait_ge(borders, b * 2 + 3)
                settled(dve)
                normalise(b, T)

            dve.memset(far[:, 1:2], 1.0).then_inc(far_sum_step, 1)
            dve.wait_ge(act_tiles, IMAGES * ACT_TILES + RING + 1)
            dve.tensor_reduce(far[:, 0:1], excess[:].rearrange("p b t -> p (b t)"), AX.X, ALU.add).then_inc(far_sum_step, 1)
            dve.wait_ge(far_sum_step, 2)
            dve.nop().then_inc(far_sum, 1)
            dve.wait_ge(far_total, 1)
            dve.tensor_scalar(flag[:], psum[0:1, STAT_BANK, 0:1], 0.0, None, ALU.is_gt).then_inc(flag_set, 1)

            def hats(s, n):
                dve.wait_ge(dist_abs, UNITS * s + (n + 1))
                d = dist_at(s, n)
                dve.tensor_scalar(d, d, 1.0, 1.0, ALU.min, ALU.subtract).then_inc(hats_made, 1)

            def product(s, j, n, first=False):
                b, k = divmod(n, TAPS)
                if n == DVE_UNITS[0] and not first:
                    dve.wait_ge(vals_made, GROUPS * (s - 1))
                dve.wait_ge(hats_made, UNITS * s + (n + 1))
                d = dist_at(s, n)
                dve.tensor_tensor(hat[:, j, b, k, :], d[:, 0, :], d[:, 1, :], ALU.mult).then_inc(prod_dve, 1)

            def take_values(s, j, g, first=False):
                if g == 0 and not first:
                    dve.wait_ge(strip_conv, s - 1)
                dve.wait_ge(vals_made, GROUPS * s + (g + 1))
                p0, p1 = GROUP * g, min(PATCHES, GROUP * (g + 1))
                w = TAPS * PS * PS
                src = psum[:, VAL_BANKS[g % 3], 0:w * (p1 - p0)].rearrange("c (p k y) -> c p k y", k=TAPS, y=PS * PS)
                dve.tensor_copy(val[:, j, :, p0:p1, :].rearrange("c k p y -> c p k y"), src).then_inc(vals_taken, 1)

            def strip_result(s, j, uses):
                dve.wait_ge(strip_conv, s + 1)
                dve.wait_ge(x1_in[j], uses * 16)
                dve.wait_ge(out_done[j], MARGIN + ((uses - 1) * 16))
                rows = lambda t: t[:, j, :].rearrange("c (i two w) -> c two i w", two=2, w=W0)
                dve.tensor_tensor(rows(outt), psum[:, SUM_BANK, :].rearrange("c (two i w) -> c two i w", two=2, w=W0),
                                  rows(x1t), ALU.add).then_inc(strip_sum, 1)

            def strip_step(s, j, uses, first=False, second=False, last=False):
                for n in range(UNITS):
                    if not last:
                        hats(s + 1, n)
                        if n - 1 in DVE_UNITS:
                            product(s + 1, 1 - j, n - 1, first)
                        if n == UNITS - 1 and n in DVE_UNITS:
                            product(s + 1, 1 - j, n, first)
                    for g in range(GROUPS):
                        if g * UNITS // GROUPS == n:
                            take_values(s, j, g, first or second)
                    if n == 13 and not first:
                        strip_result(s - 1, 1 - j, uses if j else uses - 1)

            for n in range(UNITS):
                hats(0, n)
                if n in DVE_UNITS:
                    product(0, 0, n, True)
            strip_step(0, 0, 1, first=True)
            strip_step(1, 1, 1, second=True)
            with dve.Fori(1, STRIPS // 2 - 1) as h:
                strip_step(2 * h, 0, h + 1)
                strip_step(2 * h + 1, 1, h + 1)
            strip_step(STRIPS - 2, 0, STRIPS // 2)
            strip_step(STRIPS - 1, 1, STRIPS // 2, last=True)
            strip_result(STRIPS - 1, 1, STRIPS // 2)

            G_STEPS = 1 + 5 * CHUNKS

            def g_unit(b, t, opar, u):
                with dve.Fori(0, TAPS) as k:
                    tap = u * TAPS + k

                    def step(n):
                        dve.wait_ge(g_step, tap * G_STEPS + n)

                    dve.wait_ge(g_abs, ONE + (2 * tap + 2))
                    dve.tensor_scalar(g_hat_x[:], g_hat_x[:], 1.0, 1.0, ALU.min, ALU.subtract).then_inc(g_step, 1)
                    step(1)
                    settled(dve)
                    with dve.Fori(0, CHUNKS) as y:
                        for r in range(YSTEP):
                            ins = dve.tensor_scalar(g_t[:, r, :], g_y[:], float(r), None, ALU.subtract)
                        ins.then_inc(g_step, 1)
                        step(5 * y + 2)
                        dve.scalar_tensor_tensor(out=g_t[:], in0=g_t[:], scalar=-1.0, in1=g_t[:], op0=ALU.mult,
                                                 op1=ALU.max).then_inc(g_step, 1)
                        step(5 * y + 3)
                        dve.tensor_scalar(g_t[:], g_t[:], 1.0, 1.0, ALU.min, ALU.subtract).then_inc(g_step, 1)
                        dve.tensor_scalar(g_y[:], g_y[:], float(YSTEP), None, ALU.subtract).then_inc(g_step, 1)
                        step(5 * y + 5)
                        dve.wait_ge(g_sampled, ONE + (tap * CHUNKS + y))
                        for r in range(YSTEP):
                            ins = dve.tensor_tensor(g_hat[:, r, :], g_t[:, r, :], g_hat_x[:], ALU.mult)
                        ins.then_inc(g_hats, 1)
                        dve.wait_ge(g_hats, ONE + (tap * CHUNKS + y + 1))
                        dve.nop().then_inc(g_step, 1)
                    dve.wait_ge(g_sampled, ONE + (tap * CHUNKS + CHUNKS))
                    dve.wait_ge(g_conv, ONE + (tap))
                    dve.tensor_copy(g_val[:], psum[0:CH, 2, :]).then_inc(g_taken, 1)
                dve.wait_ge(g_conv, ONE + (u * TAPS + TAPS))
                dve.wait_ge(g_x1_in, u * 16 + 16)
                dve.wait_ge(g_stored, MARGIN + (u * 16))
                dve.tensor_tensor(g_out[:], psum[0:CH, 3, :], g_x1[:], ALU.add).then_inc(g_sum, 1)

            dve.wait_ge(strip_sum, STRIPS)
            general(dve, g_unit)

        @block.gpsimd
        def _(pool):
            def border(lvl):
                L, M, C = lvl
                last = L.pitch - 1
                pool.memset(M[:, :, 0:L.pitch:last], 0.0)
                pool.memset(C[:, :, 0:L.pitch:last], 0.0)
                return pool.memset(C[:, 1:L.pairs + 1:L.pairs - 1, 1:last], 0.0)

            pool.memset(zeros[:], 0.0).then_inc(zeros_set, 1)
            pool.nop().then_inc(off_split, 2)
            pool.wait_ge(zeros_set, 1)
            margins(pool, parts_out)
            border(T).then_inc(borders, 1)
            with pool.Fori(0, IMAGES) as b:
                pool.wait_ge(pe_tiles, b * PE_TILES + PE_AT["e1b0c1"])
                settled(pool)
                for lvl in (HX, HT, QX, QT):
                    ins = border(lvl)
                ins.then_inc(borders, 1)
                pool.wait_ge(pe_tiles, b * PE_TILES + PE_AT["off"])
                settled(pool)
                border(T).then_inc(borders, 1)
                for it in loop(pool, 0, 8):
                    for s in range(2):
                        pool.wait_ge(dve_tiles, b * DVE_TILES + (2 * it + (RING + DVE_AT["norm2"] + s + 1)))
                        pool.wait_ge(turn_done, b * 16 + (2 * it + (s + 1)))
                        pool.tensor_copy(turn_in[:, s, :].rearrange("p (r w) -> p r w", w=128),
                                         tm[:, bass.ds(8 * it + 4 * s, 4), 1:129]).then_inc(turn_copied, 1)
                        pool.wait_ge(act_tiles, b * ACT_TILES + (2 * it + (RING + ACT_AT["off"] + s + 1)))

                        def step(k):
                            pool.wait_ge(pool_step, b * 48 + (6 * it + (3 * s + k)))
                            settled(pool)

                        pool.tensor_tensor(offr[:, s, :], off32[:, s, :], offp[:, s, 0, :], ALU.subtract).then_inc(pool_step, 1)
                        step(1)
                        pool.tensor_copy(offp[:, s, 1, :], offr[:, s, :]).then_inc(pool_step, 1)
                        step(2)
                        pool.tensor_tensor(offp[:, s, 2, :], offr[:, s, :], offp[:, s, 1, :], ALU.subtract).then_inc(pool_step, 1)
                        step(3)
                        for opar in range(2):
                            dst = offd[bass.ds(b, 1), bass.ds(2 * it + s, 1), :, :, opar]
                            pool.dma_start(dst.rearrange("b t c p w -> (b t c) p w"),
                                           offp[ODD_AT * opar:ODD_AT * opar + OFFC, s]).then_inc(parts_out[s], 16)
                        pool.nop().then_inc(off_split, 1)

            def products(s, j, first=False):
                if not first:
                    pool.wait_ge(vals_made, GROUPS * (s - 1))
                for n in POOL_UNITS:
                    b, k = divmod(n, TAPS)
                    pool.wait_ge(hats_made, UNITS * s + (n + 1))
                    d = dist_at(s, n)
                    pool.tensor_tensor(hat[:, j, b, k, :], d[:, 0, :], d[:, 1, :], ALU.mult).then_inc(prod_pool, 1)

            products(0, 0, True)
            products(1, 1, True)
            with pool.Fori(1, STRIPS // 2) as h:
                products(2 * h, 0)
                products(2 * h + 1, 1)
            pool.wait_ge(strip_sum, STRIPS)
            pool.memset(g_zero[:], 0.0)
            pool.memset(g_nought[:], 0.0).then_inc(g_const, 16)
    return nc


W_DMAS = 6 * len(CONV1) + 10 + 1 + 6


def selectors():
    s = np.zeros((P, TAPS, 2, WIN, WIN), np.float32)
    place_ = np.arange(WIN, dtype=np.float32)
    for k in range(TAPS):
        ky, kx = divmod(k, K)
        s[PARTS * (2 * k + 1):PARTS * (2 * k + 2), k, 0] = 1.0
        s[PARTS * 2 * k:PARTS * (2 * k + 1), k, 1] = 1.0
        s[BC_K - 3, k, 0] = 1.0
        s[BC_K - 2, k, 1] = 1.0
        s[BC_K - 1, k, 0] = (kx - 1 + HALO - place_)[None, :]
        s[BC_K - 1, k, 1] = (ky - 1 + HALO - place_)[:, None]
    out = np.zeros((P, 2 * TAPS, P), np.float32)
    out[:, :, 0:WPX] = s.reshape(P, 2 * TAPS, WPX)
    return out.astype(np.dtype("bfloat16"))


def ramps():
    r = np.ones((P - (BC_K - 3), 2, 2 * PS // 2, W0), np.float32)
    r[0] = np.arange(W0) % PS
    for par in range(2):
        for i in range(PS):
            r[1, par, i] = (2 * i + par) % PS
    return r.reshape(P - (BC_K - 3), 2 * BANK).astype(np.dtype("bfloat16"))


def column_selectors():
    s = np.zeros((BC_K, TAPS, 2, P), np.float32)
    for k in range(TAPS):
        ky, kx = divmod(k, K)
        s[PARTS * (2 * k + 1):PARTS * (2 * k + 2), k, 0] = 1.0
        s[PARTS * 2 * k:PARTS * (2 * k + 1), k, 1] = 1.0
        s[BC_K - 3, k, 0] = 1.0
        s[BC_K - 2, k, 1] = 1.0
        s[BC_K - 1, k, 0] = kx - 1 - np.arange(P)
        s[BC_K - 1, k, 1] = ky - 1
    return s.reshape(BC_K, 2 * TAPS, P).astype(np.dtype("bfloat16"))


def places():
    r = np.ones((TILES8, 2, 3, 4, W0), np.float32)
    r[:, :, 0] = np.arange(W0)
    rows = 8 * np.arange(TILES8)[:, None, None] + 2 * np.arange(4)[None, None, :] + np.arange(2)[None, :, None]
    r[:, :, 1] = rows[..., None]
    return r.reshape(TILES8, 2, 3, BANK).astype(np.dtype("bfloat16"))


def kernel(**inputs):
    import concourse.bacc as bacc
    from concourse.bass_utils import run_bass_kernel_spmd

    L0, L1 = "L0_conv_", "L1_conv_"
    by_in = lambda name: np.transpose(inputs[L0 + name], (1, 2, 3, 0))
    boff = np.zeros((50, 2), np.float32)
    boff[:, 1] = -(REACH - 2.0 ** -6)
    boff[0:OFFC, 0] = inputs[L1 + "b_off"]
    boff[ODD_AT:ODD_AT + OFFC, 0] = inputs[L1 + "b_off"]
    part = np.arange(P)
    same_group = (part[:, None] % CH) // 2 == (part[None, :] % CH) // 2
    wdef = np.zeros((P, TAPS, P), np.float32)
    for half in (slice(0, CH), slice(CH, P)):
        wdef[half, :, half] = np.transpose(inputs[L1 + "w_def"], (1, 2, 3, 0)).reshape(CH, TAPS, CH)
    arrays = {
        "x": inputs["x"],
        "w1": np.stack([by_in(n) for n in CONV1], 1),
        "w2": np.stack([by_in(n) for n in CONV2], 1),
        "wds": np.stack([by_in(n)[:, 0, 0] for n in ("e1b0ds", "e2b0ds")], 1),
        "wdec": np.stack([np.transpose(inputs[L0 + n], (0, 3, 2, 1)).reshape(CH, 2, 2 * CH) for n in ("dec0w", "dec1w")], 1),
        "woff": np.transpose(inputs[L1 + "w_off"], (1, 2, 3, 0)),
        "boff": boff,
        "wdef": wdef,
        "gmat": np.where(same_group, 0.25, 0.0).astype(np.float32),
        "ident": np.eye(P, dtype=np.float32),
        "sel": selectors(),
        "ramps": ramps(),
        "selg": column_selectors(),
        "places": places(),
    }
    arrays = {n: np.ascontiguousarray(a) for n, a in arrays.items()}
    nc = bacc.Bacc("TRN2", target_bir_lowering=False, num_devices=1)
    aps = [nc.dram_tensor(n, a.shape, mybir.dt.from_np(a.dtype), kind="ExternalInput").ap() for n, a in arrays.items()]
    out = nc.dram_tensor("out", [IMAGES, CH, H0, W0], F32, kind="ExternalOutput").ap()
    build(nc, *aps, out)
    r = run_bass_kernel_spmd(nc, [arrays], core_ids=[0])
    return r.results[0]["out"]
```

```python
from contextlib import ExitStack

import numpy as np
import concourse.bass as bass
from concourse import mybir

F32 = mybir.dt.float32
BF16 = mybir.dt.bfloat16
I32 = mybir.dt.int32
ACT = mybir.ActivationFunctionType
ALU = mybir.AluOpType
AX = mybir.AxisListType

P = 128
BN_S = float(1.0 / np.sqrt(1.0 + 0.001))
IMAGES, CH, H0, W0 = 2, 64, 128, 128
BANK = 512
RING = 4
GN_EPS = 1e-5
CROSS = 3

K = 3
TAPS = K * K
PS = 4
REACH = 2
HALO = REACH + 1
WIN = PS + 2 * HALO
WPX = WIN * WIN
PHASES = PS
LEAD = 4
QUADS = W0 // PHASES + 2
WIN_GROUPS = [(max(PHASES * q - (LEAD - HALO), 0), min(PHASES * (q + 1) - (LEAD - HALO), WIN)) for q in range(3)]
PADH = H0 + 2 * HALO
STRIPS = H0 // PS
PATCHES = W0 // PS
OFFC = 2 * TAPS
PARTS = 3
BC_K = PARTS * OFFC + 3
ODD_AT = 32

CONV1 = ["e0b0c1", "e0b0c2", "e0b1c1", "e0b1c2", "e1b0c2", "e1b1c1", "e1b1c2", "e2b0c2", "e2b1c1", "e2b1c2"]
CONV2 = ["e1b0c1", "e2b0c1"]

UNITS = IMAGES * TAPS
DIST_RING = 6
POOL_UNITS = [n for n in range(UNITS) if n % 6 != 5]
DVE_UNITS = [n for n in range(UNITS) if n % 6 == 5]
GROUP = 3
GROUPS = -(-PATCHES // GROUP)
FIRST_GROUP_AT = UNITS - GROUPS
TAP_PAIRS = -(-TAPS // 2)
FIRST_WEIGHED_AT = FIRST_GROUP_AT - TAP_PAIRS
ACT_GROUPS = [0, 2, 4, 7, 10]
DVE_GROUPS = [g for g in range(GROUPS) if g not in ACT_GROUPS]
SUM_BANK = 6
VAL_BANKS = (4, 5, 7)

YSTEP = 8
CHUNKS = H0 // YSTEP
TILES8 = H0 // 8


class Level:

    def __init__(self, side):
        self.side = side
        self.pairs = side // 2
        self.pitch = side + 2
        self.rows = BANK // side
        self.tiles = self.pairs // self.rows


FULL, HALF, QUART = Level(H0), Level(H0 // 2), Level(H0 // 4)

LAYERS = [("e0b0c1", 16), ("e0b0c2", 16), ("e0b1c1", 16), ("e0b1c2", 16), ("e1b0c1", 4), ("e1b0c2", 4), ("e1b1c1", 4),
          ("e1b1c2", 4), ("e2b0c1", 1), ("e2b0c2", 1), ("e2b1c1", 1), ("e2b1c2", 1), ("dec0", 4), ("dec1", 16), ("off", 8)]
PE_AT, PE_TILES = {}, 0
for _n, _t in LAYERS:
    PE_AT[_n] = PE_TILES
    PE_TILES += _t
DVE_AT, DVE_TILES = {}, 0
for _n, _t in [("norm1", 17), ("e0b0c2", 16), ("e0b1c2", 16), ("e1b1c2", 4), ("e2b1c2", 1), ("dec0", 4), ("dec1", 16),
               ("norm2", 17)]:
    DVE_AT[_n] = DVE_TILES
    DVE_TILES += _t
ACT_AT, ACT_TILES = {}, 0
for _n, _t in [("e0b0c1", 16), ("e0b1c1", 16), ("e1b0c1", 4), ("e1b0c2", 4), ("e1b1c1", 4), ("e2b0c1", 1), ("e2b0c2", 1),
               ("e2b1c1", 1), ("dec0", 4), ("dec1", 16), ("off", 8)]:
    ACT_AT[_n] = ACT_TILES
    ACT_TILES += _t


def loop(eng, start, end):
    if end - start == 1:
        yield start
    elif end > start:
        with eng.Fori(start, end) as i:
            yield i


def build(nc, x, w1, w2, wds, wdec, woff, boff, wdef, wtaps, gmat, ident, sel, rampc, selg, places, out):
    es = ExitStack()
    with es:
        E = es.enter_context
        at = 0

        def place(name, shape, dt, offset):
            return nc.alloc_sbuf_tensor_at(name, shape, dt, offset=offset)

        def size(shape, dt):
            n = 4 if dt in (F32, I32) else 2
            for s in shape[1:]:
                n *= s
            return (n + 31) // 32 * 32

        class Map:

            def __init__(self, start):
                self.at = start

            def __call__(self, name, shape, dt=F32):
                t = place(name, shape, dt, self.at)
                self.at += size(shape, dt)
                assert self.at <= LIMIT, (name, self.at)
                return t

        LIMIT = nc.sbuf_usable_end

        base = (nc.sbuf_base + 31) // 32 * 32
        arena = E(nc.sbuf_tensor("arena", [P, (LIMIT - base) // 4 - 8], F32))

        m = Map(base)
        excess = m("excess", [P, IMAGES, 8])
        far = m("far", [P, 2])
        flag = m("flag", [1, 1], I32)
        maps_start = m.at
        xm, xc = m("xm", [P, 64, 130]), m("xc", [P, 66, 130])
        t_start = m.at
        tm, tc = m("tm", [P, 64, 130]), m("tc", [P, 66, 130])
        h = Map(t_start)
        hxm, hxc = h("hxm", [P, 32, 66]), h("hxc", [P, 34, 66])
        htm, htc = h("htm", [P, 32, 66]), h("htc", [P, 34, 66])
        qxm, qxc = h("qxm", [P, 16, 34]), h("qxc", [P, 18, 34])
        qtm, qtc = h("qtm", [P, 16, 34]), h("qtc", [P, 18, 34])
        work_end = m.at
        w1s = m("w1s", [P, len(CONV1), 6, 128])
        w2s = m("w2s", [P, 2, 6, CH])
        wdss = m("wdss", [P, 2, CH])
        wdecs = m("wdecs", [P, 2, 4, 128])
        woffs = m("woffs", [P, 6, CH])
        split = Map(m.at)
        raw = m("raw", [P, 2, 16, 128])
        turn = Map(m.at)
        tmp = m("tmp", [P, 4, BANK])
        turned = turn("turned", [P, 2, 2, BANK])
        off32 = split("off32", [P, 2, BANK])
        offr = split("offr", [P, 2, BANK])
        offp = split("offp", [P, 2, PARTS, BANK], BF16)
        offa = m("offa", [P, BANK])
        boffs = m("boffs", [P, 2])
        gmats = m("gmats", [P, 128])
        idents = m("idents", [P, 128])
        stats = m("stats", [P, 16, 6])
        mv = m("mv", [P, 2])
        gn = m("gn", [P, 12])
        zeros = m("zeros", [P, 256])

        m2 = Map(maps_start)
        sels = m2("sels", [P, 2 * TAPS, P], BF16)
        wdefs = m2("wdefs", [P, TAP_PAIRS, CH])
        offs = m2("offs", [P, 2, IMAGES, 2, BANK], BF16)
        win = m2("win", [P, 2, IMAGES, PATCHES, CH])
        dist = m2("dist", [P, DIST_RING, 2, BANK])
        hat = m2("hat", [P, 2, IMAGES, TAPS, BANK])
        val = m2("val", [P, 2, IMAGES, TAP_PAIRS, PATCHES, PS * PS])
        x1t = m2("x1t", [P, 2, BANK])
        outt = m2("outt", [P, 2, BANK])

        m3 = Map(maps_start)
        g_sel = m3("g_sel", [BC_K, 2 * TAPS, P], BF16)
        g_wdef = m3("g_wdef", [CH, TAPS, CH])
        g_zero = m3("g_zero", [P, CH])
        g_nought = m3("g_nought", [P, BANK])
        g_offs = m3("g_offs", [BC_K, BANK], BF16)
        g_rows = m3("g_rows", [P, YSTEP, CH])
        g_hat_x = m3("g_hat_x", [P, BANK])
        g_y = m3("g_y", [P, BANK])
        g_t = m3("g_t", [P, YSTEP, BANK])
        g_hat = m3("g_hat", [P, YSTEP, BANK])
        g_val = m3("g_val", [CH, BANK])
        g_x1 = m3("g_x1", [CH, BANK])
        g_out = m3("g_out", [CH, BANK])

        X, T = (FULL, xm, xc), (FULL, tm, tc)
        HX, HT = (HALF, hxm, hxc), (HALF, htm, htc)
        QX, QT = (QUART, qxm, qxc), (QUART, qtm, qtc)

        psum = E(nc.psum_tensor("psum", [P, 8, BANK], F32))
        TURN_BANK, STAT_BANK = RING, RING + 2

        def sem(name):
            return E(nc.semaphore(name))

        w_first = sem("w_first")
        w_in = sem("w_in")
        c_in = sem("c_in")
        x_in = [sem(f"x_in{q}") for q in range(4)]
        raw_in = [sem(f"raw_in{q}") for q in range(2)]
        x1_out = sem("x1_out")
        pe_tiles = sem("pe_tiles")
        act_tiles = sem("act_tiles")
        dve_tiles = sem("dve_tiles")
        dve_step = sem("dve_step")
        stat_cols = sem("stat_cols")
        stat_sum = sem("stat_sum")
        var_ready = sem("var_ready")
        root_ready = sem("root_ready")
        cross_made = sem("cross_made")
        stats_in = sem("stats_in")
        rows_free = sem("rows_free")
        freed = sem("freed")
        raw_added = sem("raw_added")
        final_rows = sem("final_rows")
        borders = sem("borders")
        turn_done = sem("turn_done")
        turn_taken = sem("turn_taken")
        pm_out = [sem(f"pm_out{i}") for i in range(2)]
        off_ready = sem("off_ready")
        pool_step = sem("pool_step")
        off_split = sem("off_split")
        parts_out = [sem(f"parts_out{i}") for i in range(2)]

        sel_in = sem("sel_in")
        offs_in = [sem(f"offs_in{i}") for i in range(2)]
        win_in = [sem(f"win_in{i}") for i in range(2)]
        x1_in = [sem(f"x1_in{i}") for i in range(2)]
        dist_made = sem("dist_made")
        dist_abs = sem("dist_abs")
        hats_made = sem("hats_made")
        prod_pool = sem("prod_pool")
        prod_dve = sem("prod_dve")
        vals_made = sem("vals_made")
        vals_dve = sem("vals_dve")
        vals_act = sem("vals_act")
        strip_conv = sem("strip_conv")
        strip_sum = sem("strip_sum")
        out_done = [sem(f"out_done{i}") for i in range(2)]

        excess_done = sem("excess_done")
        carried = sem("carried")
        zeros_set = sem("zeros_set")
        far_sum = sem("far_sum")
        far_sum_step = sem("far_sum_step")
        far_total = sem("far_total")
        flag_set = sem("flag_set")
        g_const = sem("g_const")
        g_offs_in = sem("g_offs_in")
        g_x1_in = sem("g_x1_in")
        g_rows_in = sem("g_rows_in")
        g_dist = sem("g_dist")
        g_abs = sem("g_abs")
        g_step = sem("g_step")
        g_hats = sem("g_hats")
        g_sampled = sem("g_sampled")
        g_taken = sem("g_taken")
        g_conv = sem("g_conv")
        g_sum = sem("g_sum")
        g_stored = sem("g_stored")

        MARGIN_SEMS = [x1_out, *pm_out, *out_done, g_stored, *parts_out]
        MARGIN, ONE = 16, 1
        ONE_SEMS = [final_rows, raw_added, g_hats, g_conv, g_sampled, g_abs, g_sum, g_taken]

        x1d = nc.dram_tensor("x1d", [IMAGES, CH, H0, W0], F32, kind="Internal").ap()
        pixd = nc.dram_tensor("pixd", [IMAGES, PADH, PHASES, QUADS, CH], F32, kind="Internal").ap()
        offd = nc.dram_tensor("offd", [IMAGES, TILES8, 2, ODD_AT, PARTS, BANK], BF16, kind="Internal").ap()

        RELU, IDENT = ACT.Relu, ACT.Identity

        def bank(b):
            return psum[:, b, :]

        def by_rows(ap, level):
            return ap.rearrange("p (r w) -> p r w", w=level.side)

        def margins(eng):
            n = 0
            for b in range(IMAGES):
                for row, quad in ((0, 0), (HALO + H0, QUADS - 1)):
                    above = pixd[b, row:row + HALO].rearrange("r s q c -> (r s q c)").rearrange("(p f) -> p f", p=P)
                    eng.dma_start(above, zeros[:, 0:above.shape[1]]).then_inc(MARGIN_SEMS[n], MARGIN)
                    beside = pixd[b, HALO:HALO + H0, :, quad, :]
                    eng.dma_start(beside, zeros[:].rearrange("r (s c) -> r s c", c=CH)).then_inc(MARGIN_SEMS[n + 1], MARGIN)
                    n += 2

        def settled(eng):
            eng.sem_inc(carried, 1)

        def general(eng, unit, end=None):
            eng.wait_ge(flag_set, 1)
            wanted = eng.value_load(flag[0:1, 0:1], min_val=0, max_val=1)
            with eng.If(wanted > 0):
                with eng.Fori(0, IMAGES) as b:
                    with eng.Fori(0, TILES8) as t:
                        for opar in range(2):
                            unit(b, t, opar, b * (2 * TILES8) + (2 * t + opar))
                if end is not None:
                    end()

        def group_taken(s, g):
            counted, mine = (vals_act, ACT_GROUPS) if g in ACT_GROUPS else (vals_dve, DVE_GROUPS)
            return counted, len(mine) * s + (mine.index(g) + 1)

        def copy_group(s, j, g, copy):
            p0, p1 = GROUP * g, min(PATCHES, GROUP * (g + 1))
            w = TAPS * PS * PS
            for b in range(IMAGES):
                for odd in range(2):
                    src = psum[CH * b:CH * b + CH, VAL_BANKS[g % 3], 0:w * (p1 - p0)]
                    src = src.rearrange("c (p k y) -> c p k y", k=TAPS, y=PS * PS)[:, :, odd::2, :]
                    dst = val[CH * odd:CH * odd + CH, j, b, 0:TAP_PAIRS - odd, p0:p1, :]
                    ins = copy(dst.rearrange("c k p y -> c p k y"), src)
            return ins

        def dist_at(s, n):
            return dist[:, n % DIST_RING]

        assert UNITS % DIST_RING == 0

        block = E(nc.Block())

        @block.sync
        def _(sp):
            def load_x(b, q):
                sp.wait_ge(rows_free, b * 4 + q + 1)
                if not (isinstance(b, int) and b == 0):
                    sp.wait_ge(x1_out, MARGIN + (b * 8 * 16))
                for par in range(2):
                    src = x[bass.ds(b, 1), :, 32 * q + par:32 * q + 32:2, :].rearrange("b c r w -> (b c) r w")
                    sp.dma_start(xm[64 * par:64 * par + 64, 16 * q:16 * q + 16, 1:129], src).then_inc(x_in[q], 16)

            def raw_rows(b, q):
                if q >= 2:
                    sp.wait_ge(raw_added, ONE + (b * 4 + q - 1))
                else:
                    sp.wait_ge(raw_added, ONE + (b * 4))
                    settled(sp)
                    for s in range(2):
                        sp.wait_ge(parts_out[s], MARGIN + (b * 64))
                for par in range(2):
                    src = x[bass.ds(b, 1), :, 32 * q + par:32 * q + 32:2, :].rearrange("b c r w -> (b c) r w")
                    sp.dma_start(raw[64 * par:64 * par + 64, q % 2], src).then_inc(raw_in[q % 2], 16)

            def store_parts(b, n):
                sp.wait_ge(off_split, b * 8 + (n + 3))
                dst = offd[bass.ds(b, 1), 2 * n:2 * n + 2].rearrange("b t o c p w -> (b t o c) p w")
                sp.dma_start(dst, offp[:, n % 2]).then_inc(parts_out[n % 2], 16)

            def store_pixels(b, n):
                sp.wait_ge(turn_taken, b * 16 + (2 * n + 4))
                for phase in range(PHASES):
                    dst = pixd[bass.ds(b, 1), 16 * n + HALO:16 * n + HALO + 16, phase, 1:1 + PATCHES, :]
                    src = turned[phase::PHASES, n % 2].rearrange("w t (r c) -> w (t r) c", c=CH)
                    sp.dma_start(dst.rearrange("b r w c -> w (b r) c"), src).then_inc(pm_out[n % 2], 16)

            def x1_rows(b, q):
                sp.wait_ge(final_rows, ONE + (b * 4 + q + 1))
                for par in range(2):
                    dst = x1d[bass.ds(b, 1), :, 32 * q + par:32 * q + 32:2, :].rearrange("b c r w -> (b c) r w")
                    sp.dma_start(dst, xm[64 * par:64 * par + 64, 16 * q:16 * q + 16, 1:129]).then_inc(x1_out, 16)

            def load_offs(t, slot):
                for b in range(IMAGES):
                    src = offd[b, bass.ds(t, 1), :, 0:OFFC].rearrange("t o c p n -> (t c p) o n")
                    sp.dma_start(offs[0:BC_K - 3, slot, b], src).then_inc(offs_in[slot], 16)

            def load_windows(t, j):
                for b in range(IMAGES):
                    for q, (lo, hi) in enumerate(WIN_GROUPS):
                        src = pixd[b, bass.ds(2 * PS * t + PS * j, 1), (lo + LEAD - HALO) % PHASES, q:q + PATCHES]
                        src = bass.AP(src.tensor, src.offset, [[QUADS * CH, hi - lo], [PHASES * QUADS * CH, WIN],
                                                               [1, PATCHES * CH]])
                        sp.dma_start(win[WIN * lo:WIN * hi, j, b].rearrange("w p c -> w (p c)"), src
                                     ).then_inc(win_in[j], 16)

            def load_x1(t, j):
                src = x1d[:, :, bass.ds(2 * PS * t + PS * j, PS), :].rearrange("b c r w -> (b c) (r w)")
                sp.dma_start(x1t[:, j, :], src).then_inc(x1_in[j], 16)

            def store_strip(t, j):
                sp.wait_ge(strip_sum, 2 * t + (j + 1))
                dst = out[:, :, bass.ds(2 * PS * t + PS * j, PS), :].rearrange("b c r w -> (b c) (r w)")
                sp.dma_start(dst, outt[:, j, :]).then_inc(out_done[j], 16)

            def sampling_constants():
                sp.wait_ge(rows_free, 4 * IMAGES + 4)
                sp.wait_ge(x1_out, MARGIN + IMAGES * 8 * 16)
                sp.wait_ge(pm_out[0], MARGIN + (IMAGES - 1) * 256 + 64)
                sp.wait_ge(pm_out[1], MARGIN)
                sp.wait_ge(parts_out[0], MARGIN + (IMAGES - 1) * 64 + 16)
                for margin in MARGIN_SEMS[3:]:
                    sp.wait_ge(margin, MARGIN)
                sp.dma_start(sels[:], sel).then_inc(sel_in, 16)
                for slot in range(2):
                    for b in range(IMAGES):
                        sp.dma_start(offs[BC_K - 3:P, slot, b].rearrange("c w n -> c (w n)"), rampc).then_inc(sel_in, 16)
                sp.dma_start(wdefs[:], wtaps).then_inc(sel_in, 16)
                nought = pixd[0, 0:HALO]
                n = IMAGES * PATCHES * CH
                assert n <= HALO * PHASES * QUADS * CH
                for j in range(2):
                    sp.dma_start(win[WPX:P, j].rearrange("p b q c -> p (b q c)"),
                                 bass.AP(nought.tensor, nought.offset, [[0, P - WPX], [1, n]])).then_inc(sel_in, 16)

            def image(b, then):
                for q in range(4):
                    raw_rows(b, q)
                for q in range(4):
                    x1_rows(b, q)
                for n in range(8):
                    store_pixels(b, n)
                    store_parts(b, n)
                    then(n)

            def next_x(n):
                if n < 4:
                    load_x(b + 1, n)

            def next_stage(n):
                if n == 3:
                    sampling_constants()
                elif n == 5:
                    load_offs(0, 0)
                    load_offs(1, 1)
                elif n == 7:
                    for j in range(2):
                        load_windows(0, j)

            for counted in ONE_SEMS:
                sp.sem_inc(counted, ONE)
            sp.dma_start(gmats[:], gmat).then_inc(c_in, 16)
            sp.dma_start(idents[:], ident).then_inc(c_in, 16)
            sp.dma_start(boffs[:], boff).then_inc(c_in, 16)
            sp.sem_inc(rows_free, 4)
            for q in range(4):
                load_x(0, q)
            for lo in range(1, len(CONV1), 3):
                sp.dma_start(w1s[:, lo:lo + 3], w1[:, lo:lo + 3]).then_inc(w_in, 16)
            for dst, src in ((w2s, w2), (wdss, wds), (wdecs, wdec), (woffs, woff)):
                sp.dma_start(dst[:], src).then_inc(w_in, 16)
            sp.wait_ge(zeros_set, 1)
            margins(sp)
            for b in loop(sp, 0, IMAGES - 1):
                image(b, next_x)
            image(IMAGES - 1, next_stage)
            sp.wait_ge(x1_out, MARGIN + (IMAGES * 8 * 16))
            for i in range(2):
                sp.wait_ge(pm_out[i], MARGIN + (IMAGES * 4 * 64))
                sp.wait_ge(parts_out[i], MARGIN + (IMAGES * 4 * 16))
            for margin in MARGIN_SEMS[3:]:
                sp.wait_ge(margin, MARGIN)
            sp.wait_ge(act_tiles, IMAGES * ACT_TILES + RING)
            sp.wait_ge(dve_tiles, IMAGES * DVE_TILES + RING)
            sp.wait_ge(pe_tiles, IMAGES * PE_TILES)
            sp.wait_ge(turn_done, IMAGES * 16)
            sp.wait_ge(off_split, IMAGES * 8 + 2)

            sp.sem_inc(freed, 1)
            for j in range(2):
                load_x1(0, j)

            def strip_pair(t, slot, more):
                for j in range(2):
                    if more:
                        sp.wait_ge(vals_made, GROUPS * (2 * t + (j + 1)))
                        load_windows(t + 1, j)
                    store_strip(t, j)
                    if more:
                        load_x1(t + 1, j)
                if more == 2:
                    load_offs(t + 2, slot)

            with sp.Fori(0, STRIPS // 4 - 1) as h:
                strip_pair(2 * h, 0, 2)
                strip_pair(2 * h + 1, 1, 2)
            strip_pair(STRIPS // 2 - 2, 0, 1)
            strip_pair(STRIPS // 2 - 1, 1, 0)
            for j in range(2):
                sp.wait_ge(out_done[j], MARGIN + (16 * (STRIPS // 2)))

            def g_unit(b, t, opar, u):
                sp.wait_ge(g_stored, MARGIN + (16 * u))
                src = offd[bass.ds(b, 1), bass.ds(t, 1), opar, 0:OFFC].rearrange("b t c p n -> (b t c p) n")
                sp.dma_start(g_offs[0:BC_K - 3], src).then_inc(g_offs_in, 16)
                sp.dma_start(g_offs[BC_K - 3:BC_K], places[bass.ds(t, 1), opar].rearrange("t r n -> (t r) n")
                             ).then_inc(g_offs_in, 16)
                rows = lambda d: d[bass.ds(b, 1), :, bass.ds(8 * t, 8), :].rearrange("b c (i two) w -> two (b c) i w", two=2)[opar]
                sp.dma_start(g_x1[:].rearrange("c (i w) -> c i w", w=W0), rows(x1d)).then_inc(g_x1_in, 16)
                with sp.Fori(0, TAPS) as k:
                    with sp.Fori(0, CHUNKS) as y:
                        n = u * (TAPS * CHUNKS) + (k * CHUNKS + y)
                        sp.wait_ge(g_sampled, ONE + (n))
                        for phase in range(PHASES):
                            src = pixd[bass.ds(b, 1), bass.ds(YSTEP * y + HALO, YSTEP), phase, 1:1 + PATCHES, :]
                            sp.dma_start(g_rows[PATCHES * phase:PATCHES * (phase + 1)],
                                         src.rearrange("b r w c -> w (b r) c")).then_inc(g_rows_in, 16)
                sp.wait_ge(g_sum, ONE + (u + 1))
                sp.dma_start(rows(out), g_out[:].rearrange("c (i w) -> c i w", w=W0)).then_inc(g_stored, 16)

            sp.wait_ge(strip_sum, STRIPS)
            sp.dma_start(g_sel[:], selg).then_inc(g_const, 16)
            sp.dma_start(g_wdef[:], wdef).then_inc(g_const, 16)
            def g_end():
                sp.wait_ge(g_stored, MARGIN + 16 * 2 * TILES8 * IMAGES)

            general(sp, g_unit, g_end)
            sp.wait_ge(g_const, 48)

        @block.tensor
        def _(pe):
            def after(sem_, per_image, b, n):
                pe.wait_ge(sem_, b * per_image + (n + RING))

            def own_and_prev(b, layer, prev, it, u, tiles):
                psem, pper, ptot, pT = prev
                t0 = PE_AT[layer]
                if u == 0:
                    after(psem, pper, b, ptot - 1 if pT > 2 and tiles > 1 else ptot)
                if u == 1:
                    after(psem, pper, b, ptot)
                sem_, per, base_ = (act_tiles, ACT_TILES, ACT_AT[layer]) if layer in ACT_AT else \
                    (dve_tiles, DVE_TILES, DVE_AT[layer])
                pe.wait_ge(sem_, b * per + (4 * it + (base_ + u + 1)))

            def conv3(b, layer, src, mats, prev, extra=None):
                L, M, C = src
                n = L.rows
                T_ = L.tiles
                for it in loop(pe, 0, max(T_ // 4, 1)):
                    for u in range(min(T_, 4)):
                        own_and_prev(b, layer, prev, it, u, T_)
                        i0 = (4 * it + u) * n
                        o = by_rows(bank((PE_AT[layer] + u) % RING), L)
                        todo = [(WHOLE, mats(kx), M[:, bass.ds(i0, n), kx:kx + L.side]) for kx in range(3)]
                        todo += [(WHOLE, mats(CROSS + kx), C[:, bass.ds(i0 + 1, n), kx:kx + L.side]) for kx in range(3)]
                        if extra:
                            todo += extra(i0, n)
                        emit(o, todo)

            def emit(o, todo):
                begun = []
                for j, (part, w, rows) in enumerate(todo):
                    mm = pe.matmul(o[part], w, rows, start=not (part in begun or WHOLE in begun),
                                   stop=all(part != later[0] != WHOLE for later in todo[j + 1:]), skip_group_check=True)
                    begun.append(part)
                mm.then_inc(pe_tiles, 1)

            WHOLE, HALVES = slice(0, P), (slice(0, CH), slice(CH, P))

            def halves(src, opar, j0, n, taps, Ld):
                return src.rearrange("p (j two) w -> p j two w", two=2)[:, bass.ds(j0, n), opar, taps:taps + 2 * Ld.side:2]

            def conv3_s2(b, layer, src, dst, which, prev):
                L, M, C = src
                D = dst[0]
                n = D.rows
                cross = C[:, 1:1 + L.pairs, :]
                for it in loop(pe, 0, max(D.tiles // 4, 1)):
                    for u in range(min(D.tiles, 4)):
                        own_and_prev(b, layer, prev, it, u, D.tiles)
                        j0 = (4 * it + u) * n
                        o = by_rows(bank((PE_AT[layer] + u) % RING), D)
                        todo = []
                        for kx in range(3):
                            for at_, rows in ((0, M), (CROSS, cross)):
                                for opar in range(2):
                                    todo.append((HALVES[opar], w2s[:, which, at_ + kx, :], halves(rows, opar, j0, n, kx, D)))
                        emit(o, todo)

            def ds_terms(src, which, D):
                def terms(j0, n):
                    return [(HALVES[opar], wdss[:, which, :], halves(src[1], opar, j0, n, 1, D))
                            for opar in range(2)]
                return terms

            def deconv(b, layer, src, which, prev):
                L, M, _ = src
                for it in loop(pe, 0, L.tiles):
                    for u in range(4):
                        own_and_prev(b, layer, prev, it, u, 4)
                        o = by_rows(bank((PE_AT[layer] + u) % RING), L)
                        emit(o, [(WHOLE, wdecs[:, which, u, :], M[:, bass.ds(it * L.rows, L.rows), 1:1 + L.side])])

            def group_sums(n):
                for j in range(2):
                    pe.wait_ge(stat_cols, 2 * n + (j + 1))
                    pe.matmul(psum[:, STAT_BANK, j:j + 1], gmats[:], gn[:, 4 * j:4 * j + 1],
                              start=True, stop=True).then_inc(stat_sum, 1)

            def prev_of(layer, T_):
                if layer in DVE_AT:
                    return (dve_tiles, DVE_TILES, DVE_AT[layer] + T_, T_)
                return (act_tiles, ACT_TILES, ACT_AT[layer] + T_, T_)

            def w_of(n):
                return lambda j: w1s[:, n, j, :]

            pe.wait_ge(c_in, 3 * 16)
            with pe.Fori(0, IMAGES) as b:
                group_sums(2 * b)
                pe.wait_ge(w_first, 16)
                for it in loop(pe, 0, 4):
                    for u in range(4):
                        after(dve_tiles, DVE_TILES, b, 4 * it + (u + 2))
                        pe.wait_ge(act_tiles, b * ACT_TILES + (4 * it + (u + 1)))
                        i0 = (4 * it + u) * 4
                        todo = [(WHOLE, w1s[:, 0, kx, :], xm[:, bass.ds(i0, 4), kx:kx + 128]) for kx in range(3)]
                        todo += [(WHOLE, w1s[:, 0, CROSS + kx, :], xc[:, bass.ds(i0 + 1, 4), kx:kx + 128]) for kx in range(3)]
                        emit(by_rows(bank(u), FULL), todo)
                pe.wait_ge(w_in, W_DMAS * 16)
                conv3(b, "e0b0c2", T, w_of(1), prev_of("e0b0c1", 16))
                conv3(b, "e0b1c1", X, w_of(2), prev_of("e0b0c2", 16))
                conv3(b, "e0b1c2", T, w_of(3), prev_of("e0b1c1", 16))
                conv3_s2(b, "e1b0c1", X, HT, 0, prev_of("e0b1c2", 16))
                conv3(b, "e1b0c2", HT, w_of(4), prev_of("e1b0c1", 4), ds_terms(X, 0, HALF))
                conv3(b, "e1b1c1", HX, w_of(5), prev_of("e1b0c2", 4))
                conv3(b, "e1b1c2", HT, w_of(6), prev_of("e1b1c1", 4))
                conv3_s2(b, "e2b0c1", HX, QT, 1, prev_of("e1b1c2", 4))
                conv3(b, "e2b0c2", QT, w_of(7), prev_of("e2b0c1", 1), ds_terms(HX, 1, QUART))
                conv3(b, "e2b1c1", QX, w_of(8), prev_of("e2b0c2", 1))
                conv3(b, "e2b1c2", QT, w_of(9), prev_of("e2b1c1", 1))
                deconv(b, "dec0", QX, 0, prev_of("e2b1c2", 1))
                deconv(b, "dec1", HX, 1, prev_of("dec0", 4)[:3] + (1,))
                group_sums(2 * b + 1)
                for it in range(2):
                    for u in range(4):
                        after(dve_tiles, DVE_TILES, b, 8 * it + (DVE_AT["norm2"] + 2 * u + 3))
                        pe.wait_ge(act_tiles, b * ACT_TILES + (4 * it + (ACT_AT["off"] + u + 1)))
                        todo = []
                        for kx in range(3):
                            for at_, rows, lead in ((0, tm, 0), (CROSS, tc, 1)):
                                for side in range(2):
                                    i0 = 32 * it + (8 * u + 4 * side + lead)
                                    todo.append((HALVES[side], woffs[:, at_ + kx, :], rows[:, bass.ds(i0, 4), kx:kx + 128]))
                        emit(by_rows(bank(u), FULL), todo)
                        for s in range(2):
                            n = 8 * it + (2 * u + s)
                            pe.wait_ge(turn_taken, b * 16 + (n + 1))
                            for r in range(4):
                                mm = pe.transpose(psum[:, TURN_BANK + s, 128 * r:128 * r + 128],
                                                  tm[:, 32 * it + 8 * u + 4 * s + r, 1:129], idents[:])
                            mm.then_inc(turn_done, 1)

            def distances(s, s_of, n):
                t, j = s_of
                b, k = divmod(n, TAPS)
                if n == 0:
                    pe.wait_ge(offs_in[t[1]], t[2])
                if isinstance(s, int) and s == 0 and n < 2:
                    pass
                else:
                    pe.wait_ge(dist_abs, UNITS * s + (n - 1))
                slot = n % 2
                rows = offs[:, t[1], b, :, (BANK // 2) * j:(BANK // 2) * (j + 1)]
                for axis in range(2):
                    mm = pe.matmul(psum[:, 2 * slot + axis, :].rearrange("p (w n) -> p w n", w=2),
                                   sels[:, 2 * k + axis, :], rows, start=True, stop=True)
                mm.then_inc(dist_made, 1)

            def sample_group(s, j, g):
                if g == 0:
                    if isinstance(s, int) and s == 0:
                        pe.wait_ge(freed, 1)
                    pe.wait_ge(win_in[j[0]], j[1])
                    pe.wait_ge(prod_pool, len(POOL_UNITS) * (s + 1))
                    pe.wait_ge(prod_dve, len(DVE_UNITS) * (s + 1))
                if g >= 3:
                    pe.wait_ge(*group_taken(s, g - 3))
                elif not (isinstance(s, int) and s == 0):
                    pe.wait_ge(*group_taken(s - 1, GROUPS - 1 - (GROUPS - 1 - g) % 3))
                    settled(pe)
                o = psum[:, VAL_BANKS[g % 3], :]
                last = min(PATCHES, GROUP * (g + 1))
                for q, p in enumerate(range(GROUP * g, last)):
                    w = TAPS * PS * PS
                    for b in range(IMAGES):
                        dst = o[CH * b:CH * b + CH, w * q:w * q + w].rearrange("c (k r x) -> c k r x", k=TAPS, x=PS)
                        mm = pe.matmul(dst, win[:, j[0], b, p, :],
                                       hat[:, j[0], b].rearrange("p k (r x) -> p k r x", r=PS)[:, :, :, PS * p:PS * p + PS],
                                       start=True, stop=True, skip_group_check=True)
                mm.then_inc(vals_made, 1)

            def weigh(s, j, ks):
                if ks[0] == 0:
                    pe.wait_ge(vals_dve, len(DVE_GROUPS) * (s + 1))
                    pe.wait_ge(vals_act, len(ACT_GROUPS) * (s + 1))
                    if not (isinstance(s, int) and s == 0):
                        pe.wait_ge(strip_sum, s)
                        settled(pe)
                for k in ks:
                    for b in range(IMAGES):
                        mm = pe.matmul(psum[CH * b:CH * b + CH, SUM_BANK, :].rearrange("c (r p x) -> c r p x", r=PS, x=PS),
                                       wdefs[:, k, :], val[:, j, b, k].rearrange("c p (r x) -> c r p x", r=PS),
                                       start=k == 0, stop=k == TAP_PAIRS - 1, skip_group_check=True)
                if ks[-1] == TAP_PAIRS - 1:
                    mm.then_inc(strip_conv, 1)

            def strip_step(s, j, t_next, s_next):
                for n in range(UNITS):
                    if s_next is not None:
                        distances(s_next, t_next, n)
                    if n >= FIRST_GROUP_AT:
                        sample_group(s, j, n - FIRST_GROUP_AT)
                    elif n >= FIRST_WEIGHED_AT and not (isinstance(s, int) and s == 0):
                        weigh(s - 1, 1 - j[0], [n - FIRST_WEIGHED_AT])

            def quad(h, first=False, last=False):
                for r in range(4):
                    s, j = 4 * h + r, r % 2
                    win_count = (2 * h + r // 2 + 1) * (16 * len(WIN_GROUPS) * IMAGES)
                    s_next, jn = s + 1, (r + 1) % 2
                    slot = ((r + 1) // 2) % 2
                    count = (h + (1 if r < 3 else 2)) * (16 * IMAGES)
                    t_next = ((None, slot, count), jn)
                    end = last and r == 3
                    strip_step(s, (j, win_count), t_next, None if end else s_next)

            pe.wait_ge(act_tiles, IMAGES * ACT_TILES + RING)
            pe.wait_ge(sel_in, 16 * (1 + 2 * IMAGES + 1 + 2))
            for n in range(UNITS):
                distances(0, ((None, 0, 16 * IMAGES), 0), n)
                if n == 1:
                    pe.wait_ge(far_sum, 1)
                    pe.matmul(psum[0:1, STAT_BANK, 0:1], far[:, 0:1], far[:, 1:2], start=True, stop=True).then_inc(far_total, 1)
            pe.wait_ge(flag_set, 1)
            quad(0)
            with pe.Fori(1, STRIPS // 4 - 1) as h:
                quad(h)
            quad(STRIPS // 4 - 1, last=True)
            weigh(STRIPS - 1, 1, range(TAP_PAIRS))

            def g_unit(b, t, opar, u):
                pe.wait_ge(g_offs_in, u * 32 + 32)
                for k in range(TAPS):
                    tap = u * TAPS + k
                    pe.wait_ge(g_abs, ONE + (2 * tap))
                    for axis in range(2):
                        mm = pe.matmul(psum[:, axis, :], g_sel[:, 2 * k + axis, :], g_offs[:], start=True, stop=True)
                    mm.then_inc(g_dist, 1)
                    pe.wait_ge(g_taken, ONE + (tap))
                    acc = psum[0:CH, 2, :]
                    pe.matmul(acc, g_zero[:], g_nought[:], start=True, stop=False, skip_group_check=True)
                    with pe.Fori(0, CHUNKS) as y:
                        n = tap * CHUNKS + y
                        pe.wait_ge(g_rows_in, 64 * n + 64)
                        pe.wait_ge(g_hats, ONE + (n + 1))
                        for r in range(YSTEP):
                            mm = pe.matmul(acc, g_rows[:, r, :], g_hat[:, r, :], start=False, stop=False,
                                           skip_group_check=True)
                        mm.then_inc(g_sampled, 1)
                    pe.wait_ge(g_taken, ONE + (tap + 1))
                    if k == 0:
                        pe.wait_ge(g_sum, ONE + (u))
                    settled(pe)
                    pe.matmul(psum[0:CH, 3, :], g_wdef[:, k, :], g_val[:], start=k == 0, stop=k == TAPS - 1,
                              skip_group_check=True).then_inc(g_conv, 1)

            
            pe.wait_ge(g_const, 48)
            general(pe, g_unit)

        @block.scalar
        def _(act):
            def relu_rows(b, layer, dst):
                L, M, C = dst
                n = L.rows
                for it in loop(act, 0, max(L.tiles // 4, 1)):
                    for u in range(min(L.tiles, 4)):
                        act.wait_ge(pe_tiles, b * PE_TILES + (4 * it + (PE_AT[layer] + u + 1)))
                        i0 = (4 * it + u) * n
                        src = by_rows(bank((PE_AT[layer] + u) % RING), L)
                        inner = slice(1, 1 + L.side)
                        act.activation(M[:, bass.ds(i0, n), inner], src, RELU, scale=BN_S)
                        act.activation(C[0:64, bass.ds(i0, n), inner], src[0:64], RELU, scale=BN_S)
                        act.activation(C[64:128, bass.ds(i0 + 2, n), inner], src[64:128], RELU,
                                       scale=BN_S).then_inc(act_tiles, 1)

            def relu_tmp(b, layer, L, scale):
                for it in loop(act, 0, L.tiles):
                    for u in range(4):
                        act.wait_ge(pe_tiles, b * PE_TILES + (4 * it + (PE_AT[layer] + u + 1)))
                        act.wait_ge(dve_tiles, b * DVE_TILES + (4 * it + (DVE_AT[layer] + u + 1)))
                        act.activation(tmp[:, u, :], bank((PE_AT[layer] + u) % RING), RELU,
                                       scale=scale).then_inc(act_tiles, 1)

            def root(n):
                act.wait_ge(var_ready, n + 1)
                act.activation(gn[:, 6:7], gn[:, 5:6], ACT.Sqrt).then_inc(root_ready, 1)

            act.dma_start(w1s[:, 0], w1[:, 0]).then_inc(w_first, 16)
            act.nop().then_inc(act_tiles, RING)
            act.nop().then_inc(turn_taken, 2)
            act.wait_ge(c_in, 3 * 16)
            with act.Fori(0, IMAGES) as b:
                root(2 * b)
                act.wait_ge(borders, b * 2 + 1)
                relu_rows(b, "e0b0c1", T)
                relu_rows(b, "e0b1c1", T)
                act.wait_ge(borders, b * 2 + 2)
                relu_rows(b, "e1b0c1", HT)
                relu_rows(b, "e1b0c2", HX)
                relu_rows(b, "e1b1c1", HT)
                relu_rows(b, "e2b0c1", QT)
                relu_rows(b, "e2b0c2", QX)
                relu_rows(b, "e2b1c1", QT)
                for s in range(2):
                    act.wait_ge(pm_out[s], MARGIN + (b * 256))
                relu_tmp(b, "dec0", QUART, BN_S)
                relu_tmp(b, "dec1", HALF, BN_S * BN_S)
                root(2 * b + 1)
                for it in loop(act, 0, 2):
                    for u in range(4):
                        s, uses, n = u % 2, u // 2, 4 * it + u
                        act.wait_ge(pe_tiles, b * PE_TILES + (4 * it + (PE_AT["off"] + u + 1)))
                        act.wait_ge(off_split, b * 8 + (n + 1))
                        act.wait_ge(parts_out[s], MARGIN + (b * 64 + (32 * it + 16 * uses)))
                        act.activation(off32[:, s, :], bank(u), IDENT, bias=boffs[:, 0:1])
                        act.activation(offp[:, s, 0, :], bank(u), IDENT, bias=boffs[:, 0:1])
                        act.activation(offa[:], bank(u), ACT.Abs, bias=boffs[:, 0:1]).then_inc(act_tiles, 1)
                        act.wait_ge(act_tiles, b * ACT_TILES + (4 * it + (RING + ACT_AT["off"] + u + 1)))
                        act.activation(offa[:], offa[:], RELU, bias=boffs[:, 1:2],
                                       accum_out=excess[:, bass.ds(b, 1), bass.ds(n, 1)].rearrange("p b t -> p (b t)")
                                       ).then_inc(excess_done, 1)
                        act.wait_ge(excess_done, b * 8 + (n + 1))
                        act.wait_ge(pm_out[u % 2], MARGIN + (b * 256 + (128 * it + 64 * uses)))
                        for s in range(2):
                            n = 8 * it + (2 * u + s)
                            act.wait_ge(turn_done, b * 16 + (n + 1))
                            act.activation(turned[:, u % 2, s, :], psum[:, TURN_BANK + s, :], ACT.Copy).then_inc(turn_taken, 1)

            act.wait_ge(excess_done, 8 * IMAGES)
            act.nop().then_inc(act_tiles, 1)

            def absolute(s, n, first=False):
                act.wait_ge(dist_made, UNITS * s + (n + 1))
                if n >= DIST_RING or not first:
                    m_ = n - DIST_RING
                    q = s if m_ >= 0 else s - 1
                    m_ %= UNITS
                    who, mine = (prod_pool, POOL_UNITS) if m_ in POOL_UNITS else (prod_dve, DVE_UNITS)
                    act.wait_ge(who, len(mine) * q + (mine.index(m_) + 1))
                slot = 2 * (n % 2)
                act.activation(dist_at(s, n), psum[:, slot:slot + 2, :], ACT.Abs).then_inc(dist_abs, 1)

            def strip_step(s, j, first=False, second=False, last=False):
                for n in range(UNITS):
                    if not last:
                        absolute(s + 1, n)
                    g = n - FIRST_GROUP_AT
                    if g in ACT_GROUPS:
                        if g == ACT_GROUPS[0] and not (first or second):
                            act.wait_ge(strip_conv, s - 1)
                        act.wait_ge(vals_made, GROUPS * s + (g + 1))
                        copy_group(s, j, g, lambda o, i: act.activation(o, i, ACT.Copy)).then_inc(vals_act, 1)

            for n in range(UNITS):
                absolute(0, n, True)
            strip_step(0, 0, first=True)
            strip_step(1, 1, second=True)
            with act.Fori(1, STRIPS // 2 - 1) as h:
                strip_step(2 * h, 0)
                strip_step(2 * h + 1, 1)
            strip_step(STRIPS - 2, 0)
            strip_step(STRIPS - 1, 1, last=True)

            def g_unit(b, t, opar, u):
                with act.Fori(0, TAPS) as k:
                    tap = u * TAPS + k
                    act.wait_ge(g_dist, tap + 1)
                    act.wait_ge(g_hats, ONE + (tap * CHUNKS))
                    act.activation(g_hat_x[:], psum[:, 0, :], ACT.Abs).then_inc(g_abs, 1)
                    act.activation(g_y[:], psum[:, 1, :], ACT.Copy).then_inc(g_abs, 1)

            general(act, g_unit)

        @block.vector
        def _(dve):
            def add_relu_rows(b, layer, dst, s0):
                L, M, C = dst
                n = L.rows
                for it in loop(dve, 0, max(L.tiles // 4, 1)):
                    for u in range(min(L.tiles, 4)):
                        dve.wait_ge(pe_tiles, b * PE_TILES + (4 * it + (PE_AT[layer] + u + 1)))
                        i0 = (4 * it + u) * n
                        src = by_rows(bank((PE_AT[layer] + u) % RING), L)
                        inner = slice(1, 1 + L.side)
                        rows = M[:, bass.ds(i0, n), inner]
                        dve.scalar_tensor_tensor(out=rows, in0=src, scalar=BN_S, in1=rows, op0=ALU.mult,
                                                 op1=ALU.add).then_inc(dve_step, 1)
                        dve.wait_ge(dve_step, b * STEPS + (4 * it + (s0 + u + 1)))
                        dve.tensor_scalar(C[0:64, bass.ds(i0, n), inner], M[0:64, bass.ds(i0, n), inner], 0.0, None, ALU.max)
                        dve.tensor_scalar(C[64:128, bass.ds(i0 + 2, n), inner], M[64:128, bass.ds(i0, n), inner], 0.0, None,
                                          ALU.max).then_inc(cross_made, 1)
                        dve.wait_ge(cross_made, b * CROSSES + (4 * it + (CROSS_AT[layer] + u + 1)))
                        dve.tensor_scalar(rows, rows, 0.0, None, ALU.max).then_inc(dve_tiles, 1)

            S_GN1, S_C2, S_C4, S_C8, S_C12, S_D0 = 0, 7, 23, 39, 43, 44
            S_D1 = S_D0 + 4
            S_GN2 = S_D1
            STEPS = S_GN2 + 7

            def group_stats(b, j, s0):
                def step(k):
                    dve.wait_ge(dve_step, b * STEPS + (s0 + k))

                dve.bn_aggr(mv[:], stats[:]).then_inc(dve_step, 1)
                step(1)
                dve.tensor_copy(gn[:, 0:1], mv[:, 0:1]).then_inc(stat_cols, 1)
                dve.wait_ge(stat_sum, 4 * b + (2 * j + 1))
                dve.tensor_copy(gn[:, 2:3], psum[:, STAT_BANK, 0:1]).then_inc(dve_step, 1)
                step(2)
                dve.tensor_tensor(gn[:, 1:2], mv[:, 0:1], gn[:, 2:3], ALU.subtract).then_inc(dve_step, 1)
                step(3)
                dve.scalar_tensor_tensor(out=gn[:, 4:5], in0=gn[:, 1:2], scalar=gn[:, 1:2], in1=mv[:, 1:2], op0=ALU.mult,
                                         op1=ALU.add).then_inc(stat_cols, 1)
                dve.wait_ge(stat_sum, 4 * b + (2 * j + 2))
                dve.tensor_scalar(gn[:, 5:6], psum[:, STAT_BANK, 1:2], GN_EPS, None, ALU.add).then_inc(var_ready, 1)
                dve.wait_ge(root_ready, 2 * b + (j + 1))
                dve.reciprocal(gn[:, 7:8], gn[:, 6:7]).then_inc(dve_step, 1)
                step(4)
                dve.scalar_tensor_tensor(out=gn[:, 8:9], in0=gn[:, 7:8], scalar=gn[:, 7:8], in1=gn[:, 5:6], op0=ALU.mult,
                                         op1=ALU.mult).then_inc(dve_step, 1)
                step(5)
                dve.tensor_scalar(gn[:, 8:9], gn[:, 8:9], -0.5, 1.5, ALU.mult, ALU.add).then_inc(dve_step, 1)
                step(6)
                dve.tensor_tensor(gn[:, 9:10], gn[:, 7:8], gn[:, 8:9], ALU.mult).then_inc(dve_step, 1)
                step(7)
                settled(dve)

            CROSS_AT = {"norm1": 0, "e0b0c2": 16, "e0b1c2": 32, "e1b1c2": 48, "e2b1c2": 52}
            CROSSES = 53

            def normalise(b, dst):
                L, M, C = dst

                def rows(it, last):
                    i0 = it * 4
                    inner = slice(1, 129)
                    for o, s in ((C[0:64, bass.ds(i0, 4), inner], slice(0, 64)),
                                 (C[64:128, bass.ds(i0 + 2, 4), inner], slice(64, 128)),
                                 (M[:, bass.ds(i0, 4), inner], slice(0, 128))):
                        if M is xm and s.stop - s.start == 128:
                            ins.then_inc(cross_made, 1)
                            dve.wait_ge(cross_made, b * CROSSES + it + 1)
                        ins = dve.tensor_scalar(o, xm[s, bass.ds(i0, 4), inner], gn[s, 2:3], gn[s, 9:10], ALU.subtract,
                                                ALU.mult)
                    ins.then_inc(dve_tiles, 2 if last else 1)

                def quarter(q, last):
                    for u in range(4):
                        rows(4 * q + u, last and u == 3)
                    if M is tm:
                        dve.wait_ge(dve_tiles, b * DVE_TILES + (4 * q + (RING + DVE_AT["norm2"] + 4)))
                        dve.sem_inc(rows_free, 1)

                with dve.Fori(0, 3) as q:
                    quarter(q, False)
                quarter(3, True)

            def dec0_rows(b):
                for u in range(4):
                    par, l = divmod(u, 2)
                    dve.wait_ge(act_tiles, b * ACT_TILES + (RING + ACT_AT["dec0"] + u + 1))
                    rows = hxm[:, par::2, 1 + l:1 + l + 64:2]
                    dve.tensor_tensor(rows, by_rows(tmp[:, u, :], QUART), rows, ALU.add).then_inc(dve_step, 1)
                    dve.wait_ge(dve_step, b * STEPS + (S_D0 + u + 1))
                    dve.tensor_scalar(rows, rows, BN_S, None, ALU.mult).then_inc(dve_tiles, 1)

            def add_raw(b):
                dve.wait_ge(pe_tiles, b * PE_TILES + PE_AT["e1b1c1"])
                settled(dve)
                for it in loop(dve, 0, 2):
                    for half in range(2):
                        dve.wait_ge(raw_in[half], b * 64 + (32 * it + 32))
                        for c in range(4):
                            rows = xm[:, bass.ds(32 * it + (16 * half + 4 * c), 4), 1:129]
                            ins = dve.scalar_tensor_tensor(out=rows, in0=rows, scalar=BN_S, in1=raw[:, half, 4 * c:4 * c + 4, :],
                                                           op0=ALU.mult, op1=ALU.add)
                        ins.then_inc(raw_added, 1)

            def dec1_rows(b):
                dve.wait_ge(raw_added, ONE + (4 * b + 4))
                settled(dve)
                for it in loop(dve, 0, 2):
                    for half in range(2):
                        pairs = xm[:, bass.ds(32 * it + 16 * half, 16), :]
                        for u in range(4):
                            par, l = divmod(u, 2)
                            dve.wait_ge(act_tiles, b * ACT_TILES + (8 * it + (RING + ACT_AT["dec1"] + 4 * half + u + 1)))
                            rows = pairs[:, par::2, 1 + l:1 + l + 128:2]
                            dve.tensor_tensor(rows, by_rows(tmp[:, u, :], HALF), rows, ALU.add).then_inc(dve_tiles, 1)
                        dve.wait_ge(dve_tiles, b * DVE_TILES + (8 * it + (RING + DVE_AT["dec1"] + 4 * half + 4)))
                        for c in range(4):
                            rows = xm[:, bass.ds(32 * it + (16 * half + 4 * c), 4), 1:129]
                            ins = dve.bn_stats(stats[:, bass.ds(8 * it + (4 * half + c), 1), :].rearrange("p a s -> p (a s)"), rows)
                        ins.then_inc(final_rows, 1)

            dve.nop().then_inc(dve_tiles, RING)
            dve.memset(xm[:, :, 0:130:129], 0.0)
            dve.memset(xc[:, :, 0:130:129], 0.0)
            dve.memset(xc[:, 1:65:63, 1:129], 0.0)
            with dve.Fori(0, IMAGES) as b:
                for q in range(4):
                    dve.wait_ge(x_in[q], b * 32 + 32)
                    for c in range(4):
                        t = 4 * q + c
                        ins = dve.bn_stats(stats[:, t, :], xm[:, 4 * t:4 * t + 4, 1:129])
                ins.then_inc(stats_in, 1)
                dve.wait_ge(stats_in, b + 1)
                settled(dve)
                group_stats(b, 0, S_GN1)
                normalise(b, X)
                add_relu_rows(b, "e0b0c2", X, S_C2)
                add_relu_rows(b, "e0b1c2", X, S_C4)
                add_raw(b)
                add_relu_rows(b, "e1b1c2", HX, S_C8)
                add_relu_rows(b, "e2b1c2", QX, S_C12)
                dec0_rows(b)
                dec1_rows(b)
                dve.wait_ge(final_rows, ONE + (4 * b + 4))
                settled(dve)
                group_stats(b, 1, S_GN2)
                dve.wait_ge(borders, b * 2 + 3)
                settled(dve)
                normalise(b, T)

            dve.memset(far[:, 1:2], 1.0).then_inc(far_sum_step, 1)
            dve.wait_ge(act_tiles, IMAGES * ACT_TILES + RING + 1)
            dve.tensor_reduce(far[:, 0:1], excess[:].rearrange("p b t -> p (b t)"), AX.X, ALU.add).then_inc(far_sum_step, 1)
            dve.wait_ge(far_sum_step, 2)
            dve.nop().then_inc(far_sum, 1)
            dve.wait_ge(far_total, 1)
            dve.tensor_scalar(flag[:], psum[0:1, STAT_BANK, 0:1], 0.0, None, ALU.is_gt).then_inc(flag_set, 1)

            def hats(s, n):
                dve.wait_ge(dist_abs, UNITS * s + (n + 1))
                d = dist_at(s, n)
                dve.tensor_scalar(d, d, 1.0, 1.0, ALU.min, ALU.subtract).then_inc(hats_made, 1)

            def product(s, j, n, first=False):
                b, k = divmod(n, TAPS)
                if n == DVE_UNITS[0] and not first:
                    dve.wait_ge(vals_made, GROUPS * (s - 1))
                dve.wait_ge(hats_made, UNITS * s + (n + 1))
                d = dist_at(s, n)
                dve.tensor_tensor(hat[:, j, b, k, :], d[:, 0, :], d[:, 1, :], ALU.mult).then_inc(prod_dve, 1)

            def take_values(s, j, g, first=False):
                if g == DVE_GROUPS[0] and not first:
                    dve.wait_ge(strip_conv, s - 1)
                dve.wait_ge(vals_made, GROUPS * s + (g + 1))
                copy_group(s, j, g, dve.tensor_copy).then_inc(vals_dve, 1)

            def strip_result(s, j, uses):
                dve.wait_ge(strip_conv, s + 1)
                dve.wait_ge(x1_in[j], uses * 16)
                dve.wait_ge(out_done[j], MARGIN + ((uses - 1) * 16))
                rows = lambda t: t[:, j, :].rearrange("c (i two w) -> c two i w", two=2, w=W0)
                dve.tensor_tensor(rows(outt), psum[:, SUM_BANK, :].rearrange("c (two i w) -> c two i w", two=2, w=W0),
                                  rows(x1t), ALU.add).then_inc(strip_sum, 1)

            def strip_step(s, j, uses, first=False, second=False, last=False):
                for n in range(UNITS):
                    if n - FIRST_GROUP_AT in DVE_GROUPS:
                        take_values(s, j, n - FIRST_GROUP_AT, first or second)
                    if not last:
                        hats(s + 1, n)
                        if n - 1 in DVE_UNITS:
                            product(s + 1, 1 - j, n - 1, first)
                        if n == UNITS - 1 and n in DVE_UNITS:
                            product(s + 1, 1 - j, n, first)
                    if n == FIRST_GROUP_AT + 1 and not first:
                        strip_result(s - 1, 1 - j, uses if j else uses - 1)

            for n in range(UNITS):
                hats(0, n)
                if n in DVE_UNITS:
                    product(0, 0, n, True)
            dve.wait_ge(freed, 1)
            dve.memset(val[CH:P, :, :, TAP_PAIRS - 1], 0.0)
            strip_step(0, 0, 1, first=True)
            strip_step(1, 1, 1, second=True)
            with dve.Fori(1, STRIPS // 2 - 1) as h:
                strip_step(2 * h, 0, h + 1)
                strip_step(2 * h + 1, 1, h + 1)
            strip_step(STRIPS - 2, 0, STRIPS // 2)
            strip_step(STRIPS - 1, 1, STRIPS // 2, last=True)
            strip_result(STRIPS - 1, 1, STRIPS // 2)

            G_STEPS = 1 + 5 * CHUNKS

            def g_unit(b, t, opar, u):
                with dve.Fori(0, TAPS) as k:
                    tap = u * TAPS + k

                    def step(n):
                        dve.wait_ge(g_step, tap * G_STEPS + n)

                    dve.wait_ge(g_abs, ONE + (2 * tap + 2))
                    dve.tensor_scalar(g_hat_x[:], g_hat_x[:], 1.0, 1.0, ALU.min, ALU.subtract).then_inc(g_step, 1)
                    step(1)
                    settled(dve)
                    with dve.Fori(0, CHUNKS) as y:
                        for r in range(YSTEP):
                            ins = dve.tensor_scalar(g_t[:, r, :], g_y[:], float(r), None, ALU.subtract)
                        ins.then_inc(g_step, 1)
                        step(5 * y + 2)
                        dve.scalar_tensor_tensor(out=g_t[:], in0=g_t[:], scalar=-1.0, in1=g_t[:], op0=ALU.mult,
                                                 op1=ALU.max).then_inc(g_step, 1)
                        step(5 * y + 3)
                        dve.tensor_scalar(g_t[:], g_t[:], 1.0, 1.0, ALU.min, ALU.subtract).then_inc(g_step, 1)
                        dve.tensor_scalar(g_y[:], g_y[:], float(YSTEP), None, ALU.subtract).then_inc(g_step, 1)
                        step(5 * y + 5)
                        dve.wait_ge(g_sampled, ONE + (tap * CHUNKS + y))
                        for r in range(YSTEP):
                            ins = dve.tensor_tensor(g_hat[:, r, :], g_t[:, r, :], g_hat_x[:], ALU.mult)
                        ins.then_inc(g_hats, 1)
                        dve.wait_ge(g_hats, ONE + (tap * CHUNKS + y + 1))
                        dve.nop().then_inc(g_step, 1)
                    dve.wait_ge(g_sampled, ONE + (tap * CHUNKS + CHUNKS))
                    dve.wait_ge(g_conv, ONE + (tap))
                    dve.tensor_copy(g_val[:], psum[0:CH, 2, :]).then_inc(g_taken, 1)
                dve.wait_ge(g_conv, ONE + (u * TAPS + TAPS))
                dve.wait_ge(g_x1_in, u * 16 + 16)
                dve.wait_ge(g_stored, MARGIN + (u * 16))
                dve.tensor_tensor(g_out[:], psum[0:CH, 3, :], g_x1[:], ALU.add).then_inc(g_sum, 1)

            dve.wait_ge(strip_sum, STRIPS)
            general(dve, g_unit)

        @block.gpsimd
        def _(pool):
            def border(lvl):
                L, M, C = lvl
                last = L.pitch - 1
                pool.memset(M[:, :, 0:L.pitch:last], 0.0)
                pool.memset(C[:, :, 0:L.pitch:last], 0.0)
                return pool.memset(C[:, 1:L.pairs + 1:L.pairs - 1, 1:last], 0.0)

            pool.memset(zeros[:], 0.0).then_inc(zeros_set, 1)
            pool.nop().then_inc(off_split, 2)
            border(T).then_inc(borders, 1)
            with pool.Fori(0, IMAGES) as b:
                pool.wait_ge(pe_tiles, b * PE_TILES + PE_AT["e1b0c1"])
                settled(pool)
                for lvl in (HX, HT, QX, QT):
                    ins = border(lvl)
                ins.then_inc(borders, 1)
                pool.wait_ge(pe_tiles, b * PE_TILES + PE_AT["off"])
                settled(pool)
                border(T).then_inc(borders, 1)
                for it in loop(pool, 0, 4):
                    for u in range(2):
                        pool.wait_ge(act_tiles, b * ACT_TILES + (2 * it + (RING + ACT_AT["off"] + u + 1)))

                        def step(k):
                            pool.wait_ge(pool_step, b * 24 + (6 * it + (3 * u + k)))
                            settled(pool)

                        pool.tensor_tensor(offr[:, u, :], off32[:, u, :], offp[:, u, 0, :], ALU.subtract).then_inc(pool_step, 1)
                        step(1)
                        pool.tensor_copy(offp[:, u, 1, :], offr[:, u, :]).then_inc(pool_step, 1)
                        step(2)
                        pool.tensor_tensor(offp[:, u, 2, :], offr[:, u, :], offp[:, u, 1, :], ALU.subtract).then_inc(pool_step, 1)
                        step(3)
                        pool.nop().then_inc(off_split, 1)

            def products(s, j, first=False):
                if not first:
                    pool.wait_ge(vals_made, GROUPS * (s - 1))
                for n in POOL_UNITS:
                    b, k = divmod(n, TAPS)
                    pool.wait_ge(hats_made, UNITS * s + (n + 1))
                    d = dist_at(s, n)
                    pool.tensor_tensor(hat[:, j, b, k, :], d[:, 0, :], d[:, 1, :], ALU.mult).then_inc(prod_pool, 1)

            products(0, 0, True)
            products(1, 1, True)
            with pool.Fori(1, STRIPS // 2) as h:
                products(2 * h, 0)
                products(2 * h + 1, 1)
            pool.wait_ge(strip_sum, STRIPS)
            pool.memset(g_zero[:], 0.0)
            pool.memset(g_nought[:], 0.0).then_inc(g_const, 16)
    return nc


W_DMAS = -(-(len(CONV1) - 1) // 3) + 4


def blocks(w, odd_at):
    n = w.shape[3]
    m = np.zeros((P, 6, 2 * CH if n == CH else CH), np.float32)
    for par in range(2):
        for opar in range(2):
            m[CH * par:CH * par + CH, 0:3, odd_at * opar:odd_at * opar + n] = w[:, par - opar + 1]
    m[0:CH, CROSS:, odd_at:odd_at + n] = w[:, 2]
    m[CH:P, CROSS:, 0:n] = w[:, 0]
    return m


def selectors():
    s = np.zeros((P, TAPS, 2, WIN, WIN), np.float32)
    place_ = np.arange(WIN, dtype=np.float32)
    for k in range(TAPS):
        ky, kx = divmod(k, K)
        s[PARTS * (2 * k + 1):PARTS * (2 * k + 2), k, 0] = 1.0
        s[PARTS * 2 * k:PARTS * (2 * k + 1), k, 1] = 1.0
        s[BC_K - 3, k, 0] = 1.0
        s[BC_K - 2, k, 1] = 1.0
        s[BC_K - 1, k, 0] = (kx - 1 + HALO - place_)[:, None]
        s[BC_K - 1, k, 1] = (ky - 1 + HALO - place_)[None, :]
    out = np.zeros((P, 2 * TAPS, P), np.float32)
    out[:, :, 0:WPX] = s.reshape(P, 2 * TAPS, WPX)
    return out.astype(np.dtype("bfloat16"))


def ramps():
    r = np.ones((P - (BC_K - 3), 2, 2 * PS // 2, W0), np.float32)
    r[0] = np.arange(W0) % PS
    for par in range(2):
        for i in range(PS):
            r[1, par, i] = (2 * i + par) % PS
    return r.reshape(P - (BC_K - 3), 2 * BANK).astype(np.dtype("bfloat16"))


def column_selectors():
    s = np.zeros((BC_K, TAPS, 2, P), np.float32)
    for k in range(TAPS):
        ky, kx = divmod(k, K)
        s[PARTS * (2 * k + 1):PARTS * (2 * k + 2), k, 0] = 1.0
        s[PARTS * 2 * k:PARTS * (2 * k + 1), k, 1] = 1.0
        s[BC_K - 3, k, 0] = 1.0
        s[BC_K - 2, k, 1] = 1.0
        s[BC_K - 1, k, 0] = kx - 1 - np.arange(P).reshape(PATCHES, PHASES).T.reshape(P)
        s[BC_K - 1, k, 1] = ky - 1
    return s.reshape(BC_K, 2 * TAPS, P).astype(np.dtype("bfloat16"))


def places():
    r = np.ones((TILES8, 2, 3, 4, W0), np.float32)
    r[:, :, 0] = np.arange(W0)
    rows = 8 * np.arange(TILES8)[:, None, None] + 2 * np.arange(4)[None, None, :] + np.arange(2)[None, :, None]
    r[:, :, 1] = rows[..., None]
    return r.reshape(TILES8, 2, 3, BANK).astype(np.dtype("bfloat16"))


def kernel(**inputs):
    import concourse.bacc as bacc
    from concourse.bass_utils import run_bass_kernel_spmd

    L0, L1 = "L0_conv_", "L1_conv_"
    by_in = lambda name: np.transpose(inputs[L0 + name], (1, 2, 3, 0))
    boff = np.zeros((P, 2), np.float32)
    boff[:, 1] = -(REACH - 2.0 ** -6)
    for at in range(0, P, ODD_AT):
        boff[at:at + OFFC, 0] = inputs[L1 + "b_off"]
    part = np.arange(P)
    same_group = (part[:, None] % CH) // 2 == (part[None, :] % CH) // 2
    w2, wds = np.zeros((P, 2, 6, CH), np.float32), np.zeros((P, 2, CH), np.float32)
    wdec = np.zeros((P, 2, 4, P), np.float32)
    for which in range(2):
        w = by_in(CONV2[which])
        wds[0:CH, which] = by_in(("e1b0ds", "e2b0ds")[which])[:, 0, 0]
        for par in range(2):
            rows = slice(CH * par, CH * par + CH)
            w2[rows, which, 0:3] = w[:, 1 + par]
            wdec[rows, which, 2 * par:2 * par + 2] = np.transpose(
                inputs[L0 + ("dec0w", "dec1w")[which]], (0, 3, 2, 1)).reshape(CH, 2, P)
        w2[CH:P, which, CROSS:] = w[:, 0]
    wdef = np.transpose(inputs[L1 + "w_def"], (1, 2, 3, 0)).reshape(CH, TAPS, CH)
    wtaps = np.zeros((P, TAP_PAIRS, CH), np.float32)
    wtaps[0:CH] = wdef[:, 0::2]
    wtaps[CH:P, 0:TAP_PAIRS - 1] = wdef[:, 1::2]
    arrays = {
        "x": inputs["x"],
        "w1": np.stack([blocks(by_in(n), CH) for n in CONV1], 1),
        "w2": w2,
        "wds": wds,
        "wdec": wdec,
        "woff": blocks(np.transpose(inputs[L1 + "w_off"], (1, 2, 3, 0)), ODD_AT),
        "boff": boff,
        "wdef": wdef,
        "wtaps": wtaps,
        "gmat": np.where(same_group, 0.25, 0.0).astype(np.float32),
        "ident": np.eye(P, dtype=np.float32),
        "sel": selectors(),
        "ramps": ramps(),
        "selg": column_selectors(),
        "places": places(),
    }
    arrays = {n: np.ascontiguousarray(a) for n, a in arrays.items()}
    nc = bacc.Bacc("TRN2", target_bir_lowering=False, num_devices=1)
    aps = [nc.dram_tensor(n, a.shape, mybir.dt.from_np(a.dtype), kind="ExternalInput").ap() for n, a in arrays.items()]
    out = nc.dram_tensor("out", [IMAGES, CH, H0, W0], F32, kind="ExternalOutput").ap()
    build(nc, *aps, out)
    r = run_bass_kernel_spmd(nc, [arrays], core_ids=[0])
    return r.results[0]["out"]
```
